# Optimizing a Trainium2 kernel written in Bass

```python
import numpy as np
import jax
import jax.numpy as jnp

def _softmax(x, axis=-1):
    return jax.nn.softmax(x, axis=axis)
def _gelu(x):
    return jax.nn.gelu(x, approximate=True)
def _silu(x):
    return jax.nn.silu(x)
def _sigmoid(x):
    return jax.nn.sigmoid(x)
def _layernorm(x, axis=-1, eps=1e-5):
    m = jnp.mean(x, axis=axis, keepdims=True)
    v = jnp.var(x, axis=axis, keepdims=True)
    return (x - m) / jnp.sqrt(v + eps)
def _scatter_add(tgt, idx, src, axis=0):
    return tgt.at[idx].add(src)
def _segment_sum(src, seg, n):
    return jax.ops.segment_sum(src, seg, n)

kernel_name = 'mk_adj_preln_d2_adj_512_8ef3ae'

def setup_inputs(seed: int = 0):
    np.random.seed(seed)
    _w = jnp.asarray
    def _rec_inputs():
        import jax
        import jax.numpy as jnp
        _gk = jax.random.key(seed)
        x = -0.0002928 + 1 * jax.random.normal(jax.random.fold_in(_gk, 1), (64, 256, 512), jnp.float32)
        _a = jax.random.bernoulli(jax.random.fold_in(_gk, 2), 0.03125, (64, 256, 256))
        _a = jnp.logical_or(_a, jnp.swapaxes(_a, -1, -2))
        _a = jnp.logical_or(_a, jnp.eye(256, dtype=bool))
        adj = _a.astype(jnp.int32)
        return x, adj
    x, adj = _rec_inputs()
    def _L0_gnn_setup():
        import jax, jax.numpy as jnp
        import numpy as np
        ALPHA = 0.2

        def _leaky(x):
            return jnp.where(x >= 0, x, ALPHA * x)
        key = jax.random.key(seed)
        k1, k2, k3, k4 = jax.random.split(key, 4)
        B, N, F_in, F_out = (4, 2048, 512, 512)
        h = jax.random.normal(k1, (B, N, F_in), dtype=jnp.float32)
        W = jax.random.normal(k2, (F_in, F_out), dtype=jnp.float32) * 0.05
        a = jax.random.normal(k3, (2 * F_out, 1), dtype=jnp.float32) * 0.05
        adj = jax.random.randint(k4, (B, N, N), 0, 2, dtype=jnp.int32)
        return {'h': h, 'W': W, 'a': a, 'adj': adj}
    _L0_gnn_all = _L0_gnn_setup()
    _L0_gnn_in = {k: v for k, v in _L0_gnn_all.items() if k in ('W', 'a', )}
    del _L0_gnn_all

    def _L1_gnn_setup():
        import jax, jax.numpy as jnp
        import numpy as np
        EMBED_DIM = 512
        N_HEADS = 8
        HEAD_DIM = EMBED_DIM // N_HEADS
        NEG_INF = -1000000000.0
        key = jax.random.key(seed)
        ks = jax.random.split(key, 10)
        bs, n_agents = (64, 256)
        inputs = jax.random.normal(ks[0], (bs, n_agents, EMBED_DIM), dtype=jnp.float32)
        adj = jax.random.randint(ks[1], (bs, n_agents, n_agents), 0, 2, dtype=jnp.int32)
        s = 1.0 / np.sqrt(EMBED_DIM)
        Wq = jax.random.normal(ks[2], (EMBED_DIM, EMBED_DIM), dtype=jnp.float32) * s
        Wk = jax.random.normal(ks[3], (EMBED_DIM, EMBED_DIM), dtype=jnp.float32) * s
        Wv = jax.random.normal(ks[4], (EMBED_DIM, EMBED_DIM), dtype=jnp.float32) * s
        Wo = jax.random.normal(ks[5], (EMBED_DIM, EMBED_DIM), dtype=jnp.float32) * s
        bq = jnp.zeros((EMBED_DIM,), jnp.float32)
        bk = jnp.zeros((EMBED_DIM,), jnp.float32)
        bv = jnp.zeros((EMBED_DIM,), jnp.float32)
        bo = jnp.zeros((EMBED_DIM,), jnp.float32)
        return {'inputs': inputs, 'adj': adj, 'Wq': Wq, 'bq': bq, 'Wk': Wk, 'bk': bk, 'Wv': Wv, 'bv': bv, 'Wo': Wo, 'bo': bo}
    _L1_gnn_all = _L1_gnn_setup()
    _L1_gnn_in = {k: v for k, v in _L1_gnn_all.items() if k in ('Wq', 'bq', 'Wk', 'bk', 'Wv', 'bv', 'Wo', 'bo', )}
    del _L1_gnn_all

    return {
        "x": x,
        "adj": adj,
        "L0_gnn_W": _L0_gnn_in["W"],
        "L0_gnn_a": _L0_gnn_in["a"],
        "L1_gnn_Wq": _L1_gnn_in["Wq"],
        "L1_gnn_bq": _L1_gnn_in["bq"],
        "L1_gnn_Wk": _L1_gnn_in["Wk"],
        "L1_gnn_bk": _L1_gnn_in["bk"],
        "L1_gnn_Wv": _L1_gnn_in["Wv"],
        "L1_gnn_bv": _L1_gnn_in["bv"],
        "L1_gnn_Wo": _L1_gnn_in["Wo"],
        "L1_gnn_bo": _L1_gnn_in["bo"],
    }

def reference(x, adj, L0_gnn_W, L0_gnn_a, L1_gnn_Wq, L1_gnn_bq, L1_gnn_Wk, L1_gnn_bk, L1_gnn_Wv, L1_gnn_bv, L1_gnn_Wo, L1_gnn_bo):
    import jax
    import jax.numpy as jnp
    def _L0_gnn_ref(h, W, a, adj):
        import jax, jax.numpy as jnp
        import numpy as np
        ALPHA = 0.2

        def _leaky(x):
            return jnp.where(x >= 0, x, ALPHA * x)
        F_out = W.shape[1]
        Wh = jnp.matmul(h, W)
        Wh_sg = jax.lax.stop_gradient(Wh)
        a1 = a[:F_out, 0]
        a2 = a[F_out:, 0]
        s_i = Wh_sg @ a1
        s_j = Wh_sg @ a2
        e = _leaky(s_i[:, :, None] + s_j[:, None, :])
        e = jnp.where(adj > 0, e, jnp.float32(-9000000000000000.0))
        attention = jax.nn.softmax(e, axis=1)
        h_prime = jnp.einsum('bij,bjf->bif', attention, Wh)
        return _leaky(h_prime)

    def _L1_gnn_ref(inputs, adj, Wq, bq, Wk, bk, Wv, bv, Wo, bo):
        import jax, jax.numpy as jnp
        import numpy as np
        EMBED_DIM = 512
        N_HEADS = 8
        HEAD_DIM = EMBED_DIM // N_HEADS
        NEG_INF = -1000000000.0
        bs, n, _ = inputs.shape
        q = (inputs @ Wq + bq).reshape(bs, n, N_HEADS, HEAD_DIM)
        k = (inputs @ Wk + bk).reshape(bs, n, N_HEADS, HEAD_DIM)
        v = (inputs @ Wv + bv).reshape(bs, n, N_HEADS, HEAD_DIM)
        logits = jnp.einsum('bqhd,bkhd->bhqk', q, k) / np.sqrt(HEAD_DIM)
        mask = (adj > 0)[:, None, :, :]
        logits = jnp.where(mask, logits, NEG_INF)
        attn = jax.nn.softmax(logits, axis=-1)
        out = jnp.einsum('bhqk,bkhd->bqhd', attn, v).reshape(bs, n, EMBED_DIM)
        out = out @ Wo + bo
        return jax.nn.relu(out)

    h = jnp.maximum(_layernorm(x, axis=-1), 0.0)
    x = x + _L0_gnn_ref(h, L0_gnn_W, L0_gnn_a, adj)
    h = jnp.maximum(_layernorm(x, axis=-1), 0.0)
    x = x + _L1_gnn_ref(h, adj, L1_gnn_Wq, L1_gnn_bq, L1_gnn_Wk, L1_gnn_bk, L1_gnn_Wv, L1_gnn_bv, L1_gnn_Wo, L1_gnn_bo)
    return x


_drawn_inputs = setup_inputs


def setup_inputs(seed=0):
    import zlib

    import numpy as np

    out = dict(_drawn_inputs(seed))
    spreads = {'L1_gnn_bq': (0.0, 0.8),
     'L1_gnn_bk': (0.0, 0.8),
     'L1_gnn_bv': (0.0, 0.1),
     'L1_gnn_bo': (0.0, 0.1)}
    factors = {}
    for name, (base, spread) in spreads.items():
        noise = np.random.default_rng([zlib.crc32(name.encode()), seed]).standard_normal(out[name].shape)
        drawn = base * np.exp(spread * noise) if base else spread * noise
        out[name] = jnp.asarray(drawn.astype(out[name].dtype))
    for name, factor in factors.items():
        out[name] = (out[name] * factor).astype(out[name].dtype)
    return out
```

```python
from contextlib import ExitStack

import concourse.bass as bass
from concourse import mybir

F32 = mybir.dt.float32
F16 = mybir.dt.float16
BF16 = mybir.dt.bfloat16
I32 = mybir.dt.int32
ACT = mybir.ActivationFunctionType
ALU = mybir.AluOpType
AX_X = mybir.AxisListType.X

P = 128
NH = 8
EPS = 1e-5
LEAK = 0.2
MASKED = -1e30
WS = 16.0

TR_STEPS = ["T0", "PT0", "PT1", "PT2", "T1", "PT3", "OT"]
PJ_STEPS = ["WH0", "WH1", "S", "ZT", "V0", "V1", "AT0", "AT1", "WO0", "WO1", "Q0", "Q1", "K0", "K1"]
STEP_OF = {"T0": "A", "T1": "A", "OT": "C", "WH0": "A", "WH1": "A", "S": "A", "ZT": "A", "V0": "C", "V1": "C",
           "AT0": "A", "AT1": "A", "WO0": "W", "WO1": "W", "Q0": "A", "Q1": "A", "K0": "A", "K1": "A",
           "PT0": "C", "PT1": "C", "PT2": "C", "PT3": "C"}


class Iteration:

    def __init__(self, n, parity, stages, graphs):
        self.n, self.parity, self.stages = n, parity, stages
        self.tr_before, self.pj_before = self.uses_before(n, graphs)

    @staticmethod
    def uses_before(n, graphs):
        if isinstance(n, int) and n < 1:
            return {-2: (0, 0), -1: (0, 0), 0: (2, 10)}[n]
        if isinstance(n, int) and n == graphs:
            return 2 + 7 * (n - 1) + 5, 14 * (n - 1) + 8 + 4
        return 2 + 7 * n, 14 * n + 8

    def has(self, stage):
        return stage in self.stages

    def tr(self, step):
        return self.tr_before + [s for s in TR_STEPS if self.has(STEP_OF[s])].index(step)

    def pj(self, step):
        at = [s for s in PJ_STEPS if self.has(STEP_OF[s])].index(step)
        return at % 2, self.pj_before + at


def need(eng, sem, value):
    if isinstance(value, int) and value <= 0:
        return
    eng.wait_ge(sem, value)


def build(nc, x, adj, w_gat, a_gat, wq, bq, wk, bk, wv, bv, wo, bo, out):
    B, N, D = x.shape
    KC = D // P
    RT = N // P
    DH = D // NH
    SCORE = float(DH) ** -0.5 / (WS * WS)
    assert (N, D, DH) == (256, 512, 64) and B >= 6 and B % 2 == 0

    with ExitStack() as ctx:
        def sb(name, shape, dt):
            return ctx.enter_context(nc.sbuf_tensor(name, shape, dt))

        def sem(name):
            return ctx.enter_context(nc.semaphore(name))

        tr = ctx.enter_context(nc.psum_tensor("tr", [P, 2, 512], F32))
        lg = ctx.enter_context(nc.psum_tensor("lg", [P, 2, 512], F32))
        pj = ctx.enter_context(nc.psum_tensor("pj", [P, 2, 512], F32))
        o_ps = ctx.enter_context(nc.psum_tensor("o_ps", [P, RT, 512], F32))

        id32 = sb("id32", [P, P], F32)
        id16 = sb("id16", [P, P], F16)
        idbf = sb("idbf", [P, P], BF16)
        neg_half = sb("neg_half", [P, RT], F32)
        names = ("gat", "q", "k", "v", "o")
        w_dram = dict(zip(names, (w_gat, wq, wk, wv, wo)))
        w_raw = {m: sb(f"w_raw_{m}", [P, KC, D], F32) for m in names}
        w_hi = {m: sb(f"w_hi_{m}", [P, KC, D], F16) for m in names}
        w_lo = {m: sb(f"w_lo_{m}", [P, KC, D], F16) for m in names}
        a_rows = sb("a_rows", [P, 2, D], F32)
        wa = sb("wa", [P, KC, 2], F32)
        wa_hi = sb("wa_hi", [P, KC, 2], F16)
        wa_lo = sb("wa_lo", [P, KC, 2], F16)
        wa_prod = sb("wa_prod", [P, 2, D], F32)
        bias_raw = {m: sb(f"bias_raw_{m}", [P, KC], F32) for m in "qkv"}
        bias = {m: sb(f"bias_{m}", [P, KC], F32) for m in "qkv"}
        bv_hi = sb("bv_hi", [P, KC], F16)
        bv_lo = sb("bv_lo", [P, KC], F16)
        bo_rows = sb("bo_rows", [P, D], F32)
        out_bias = sb("out_bias", [P, D], F32)

        x_in = sb("x_in", [P, RT, D], F32)
        adj_in = sb("adj_in", [P, RT, N], I32)
        mask = [sb(f"mask{i}", [P, RT, N], BF16) for i in range(2)]
        stats = [sb(f"stats{i}", [P, RT, 6], F32) for i in range(2)]
        moments = [sb(f"moments{i}", [P, RT, 2], F32) for i in range(2)]
        neg_mean = [sb(f"neg_mean{i}", [P, RT], F32) for i in range(2)]
        var_eps = [sb(f"var_eps{i}", [P, RT], F32) for i in range(2)]
        shift = [sb(f"shift{i}", [P, RT], F32) for i in range(2)]
        rstd = [sb(f"rstd{i}", [P, RT], F32) for i in range(2)]
        hn = [sb(f"hn{i}", [P, RT, D], F32) for i in range(2)]
        ht_hi = [sb(f"ht_hi{i}", [P, KC, N], F16) for i in range(2)]
        ht_lo = [sb(f"ht_lo{i}", [P, KC, N], F16) for i in range(2)]

        wh_hi = sb("wh_hi", [P, RT, D], F16)
        wh_lo = sb("wh_lo", [P, RT, D], F16)
        si_hi = sb("si_hi", [P, RT], F16)
        si_lo = sb("si_lo", [P, RT], F16)
        sj_bias = sb("sj_bias", [P, RT], F32)
        z_relu = sb("z_relu", [P, RT, N], F32)
        z_e = sb("z_e", [P, RT, N], F32)
        z_negmax = sb("z_negmax", [P, RT], F32)
        z_sum = sb("z_sum", [P, RT], F32)
        z_inv = sb("z_inv", [P, RT], F32)
        z_inv16 = sb("z_inv16", [P, RT], F32)
        p0 = sb("p0", [P, RT, N], F32)
        p0_hi = sb("p0_hi", [P, RT, N], F16)
        p0_lo = sb("p0_lo", [P, RT, N], F16)
        relu_part = sb("relu_part", [P, RT, D], F32)
        leak_part = sb("leak_part", [P, RT, D], F32)
        x1 = sb("x1", [P, RT, D], F32)
        x1_kept = [sb(f"x1_kept{i}", [P, RT, D], F32) for i in range(2)]

        q_hi = sb("q_hi", [P, KC, N], F16)
        q_lo = sb("q_lo", [P, KC, N], F16)
        k_hi = sb("k_hi", [P, KC, N], F16)
        k_lo = sb("k_lo", [P, KC, N], F16)
        v_hi = sb("v_hi", [P, RT, D], F16)
        v_lo = sb("v_lo", [P, RT, D], F16)
        negmax = sb("negmax", [P, 4], F32)
        negmax_scaled = sb("negmax_scaled", [P, 4], F32)
        p_exp = sb("p_exp", [P, 4, N], F32)
        p_sum = sb("p_sum", [P, RT, NH], F32)
        p_inv = sb("p_inv", [P, RT, NH], F32)
        pt_hi = sb("pt_hi", [P, 2, 512], F16)
        pt_lo = sb("pt_lo", [P, 2, 512], F16)
        o_n = sb("o_n", [P, RT, D], F32)
        ot_hi = sb("ot_hi", [P, KC, N], F16)
        ot_lo = sb("ot_lo", [P, KC, N], F16)
        y_lin = sb("y_lin", [P, RT, D], F32)
        y_out = sb("y_out", [P, RT, D], F32)

        ident_zeroed = sem("ident_zeroed")
        ident_ready = sem("ident_ready")
        w_loaded = {m: sem(f"w_loaded_{m}") for m in names}
        a_loaded = sem("a_loaded")
        bias_loaded = sem("bias_loaded")
        w_hi_done = sem("w_hi_done")
        w_lo_done = sem("w_lo_done")
        wa_summed = sem("wa_summed")
        wa_hi_done = sem("wa_hi_done")
        wa_lo_done = sem("wa_lo_done")
        bias_scaled = sem("bias_scaled")
        bv_hi_done = sem("bv_hi_done")
        bv_lo_done = sem("bv_lo_done")
        out_bias_summed = sem("out_bias_summed")
        out_bias_done = sem("out_bias_done")
        x_loaded = sem("x_loaded")
        adj_loaded = sem("adj_loaded")
        mask_done = sem("mask_done")
        stats_done = [sem(f"stats_done{i}") for i in range(2)]
        moments_done = [sem(f"moments_done{i}") for i in range(2)]
        ln_terms = [sem(f"ln_terms{i}") for i in range(2)]
        rstd_done = [sem(f"rstd_done{i}") for i in range(2)]
        shift_done = [sem(f"shift_done{i}") for i in range(2)]
        hn_done = [sem(f"hn_done{i}") for i in range(2)]
        tr_ready, tr_hi, tr_free = sem("tr_ready"), sem("tr_hi"), sem("tr_free")
        pj_ready, pj_free = sem("pj_ready"), sem("pj_free")
        wh_hi_done = sem("wh_hi_done")
        s_hi_done = sem("s_hi_done")
        z_relu_done = sem("z_relu_done")
        z_e_done = sem("z_e_done")
        z_max_done = sem("z_max_done")
        z_exp_done = sem("z_exp_done")
        z_inv_done = sem("z_inv_done")
        z_scale_done = sem("z_scale_done")
        p0_hi_done = sem("p0_hi_done")
        p0_lo_done = sem("p0_lo_done")
        at_relu_done = sem("at_relu_done")
        x1_done = sem("x1_done")
        x1_kept_done = sem("x1_kept_done")
        qk_hi_done = sem("qk_hi_done")
        v_hi_done = sem("v_hi_done")
        lg_ready = sem("lg_ready")
        max_done = sem("max_done")
        max_scaled = sem("max_scaled")
        exp_done = sem("exp_done")
        o_ready = sem("o_ready")
        p_inv_done = sem("p_inv_done")
        o_n_done = sem("o_n_done")
        y_lin_done = sem("y_lin_done")
        y_done = sem("y_done")
        y_stored = sem("y_stored")

        x_rows = x.rearrange("b (r p) d -> b p r d", p=P)
        adj_rows = adj.rearrange("b (r p) n -> b p r n", p=P)
        out_rows = out.rearrange("b (r p) d -> b p r d", p=P)

        def every_iteration(eng, body):
            for n, stages in ((-2, "N"), (-1, "AN"), (0, "ACN")):
                body(Iteration(n, n % 2, stages, B))
            last = B - 4
            with eng.Fori(1, last + 1, 2) as i:
                for step in range(2):
                    body(Iteration(i + step, (1 + step) % 2, "ACWN", B))
            for n, stages in ((last + 1, "ACWN"), (last + 2, "ACW"), (last + 3, "CW"), (last + 4, "W")):
                body(Iteration(n, n % 2, stages, B))

        block = ctx.enter_context(nc.Block())

        @block.sync
        def _(sp):
            def load(n_graph, sp=sp):
                sp.dma_start(adj_in[:], adj_rows[n_graph]).then_inc(adj_loaded, 16)

            sp.dma_start(x_in[:], x_rows[0]).then_inc(x_loaded, 16)
            sp.dma_start(w_raw["gat"][:], w_dram["gat"].rearrange("(c p) n -> p c n", p=P)).then_inc(w_loaded["gat"], 16)
            load(0)
            a_bcast = a_gat.rearrange("(s d) one -> one s d", s=2).to_broadcast([P, 2, D])
            sp.dma_start(a_rows[:], a_bcast).then_inc(a_loaded, 16)
            for m in ("q", "k", "v", "o"):
                sp.dma_start(w_raw[m][:], w_dram[m].rearrange("(c p) n -> p c n", p=P)).then_inc(w_loaded[m], 16)
            with nc.allow_non_contiguous_dma(reason="three bias vectors, once"):
                for m, b in (("q", bq), ("k", bk), ("v", bv)):
                    sp.dma_start(bias_raw[m][:], b.rearrange("(c p) -> p c", p=P)).then_inc(bias_loaded, 16)
            sp.dma_start(bo_rows[:], bo.rearrange("(one d) -> one d", one=1).to_broadcast([P, D])).then_inc(bias_loaded, 16)

            def body(it):
                n = it.n
                f, w = n + 2, n - 1
                if it.has("N") and it.has("A"):
                    need(sp, mask_done, f)
                    sp.dma_start(adj_in[:], adj_rows[bass.ds(f, 1)].rearrange("b p r n -> p (b r) n")).then_inc(adj_loaded, 16)
                    need(sp, pj_free, it.pj("AT1")[1] + 1)
                    sp.dma_start(x_in[:], x_rows[bass.ds(f, 1)].rearrange("b p r d -> p (b r) d")).then_inc(x_loaded, 16)
                if it.has("W"):
                    need(sp, y_done, 2 * (w + 1))
                    sp.dma_start(out_rows[bass.ds(w, 1)].rearrange("b p r d -> p (b r) d"), y_out[:]).then_inc(y_stored, 16)

            every_iteration(sp, body)
            sp.wait_ge(y_stored, 16 * B)

        @block.gpsimd
        def _(pool):
            pool.memset(id32[:], 0.0).then_inc(ident_zeroed, 1)
            pool.memset(neg_half[:], -0.5).then_inc(ident_zeroed, 1)
            pool.wait_ge(ident_zeroed, 2)
            pool.affine_select(out=id32[:], in_=id32[:], compare_op=ALU.not_equal, fill=1.0, base=0,
                               pattern=[[-1, P]], channel_multiplier=1).then_inc(ident_zeroed, 1)
            pool.wait_ge(ident_zeroed, 3)
            pool.tensor_copy(id16[:], id32[:]).then_inc(ident_ready, 1)
            pool.tensor_copy(idbf[:], id32[:]).then_inc(ident_ready, 1)

            def norm_factors(ln, g):
                need(pool, ln_terms[ln], 2 * (g + 1))
                pool.tensor_tensor(rstd[ln][:], var_eps[ln][:], neg_half[:], ALU.pow).then_inc(rstd_done[ln], 1)
                need(pool, rstd_done[ln], g + 1)
                pool.tensor_tensor(shift[ln][:], neg_mean[ln][:], rstd[ln][:], ALU.mult).then_inc(shift_done[ln], 1)

            def body(it):
                n = it.n
                a, f, w = n + 1, n + 2, n - 1
                if it.has("A"):
                    for r in range(RT):
                        need(pool, pj_free, it.pj(f"AT{r}")[1] + 1)
                        need(pool, hn_done[1], 2 * a)
                        pool.tensor_tensor(x1[:, r, :], relu_part[:, r, :], leak_part[:, r, :], ALU.add).then_inc(x1_done, 1)
                    norm_factors(1, a)
                    if it.has("W"):
                        need(pool, y_done, 2 * (w + 1))
                    for r in range(RT):
                        pool.tensor_tensor(x1_kept[1 - it.parity][:, r, :], relu_part[:, r, :], leak_part[:, r, :],
                                           ALU.add).then_inc(x1_kept_done, 1)
                if it.has("N"):
                    norm_factors(0, f)

            every_iteration(pool, body)

        @block.tensor
        def _(pe):
            def to_transposed(step, it, source, ready, value):
                need(pe, ready, value)
                for bank in range(2):
                    need(pe, tr_free, 2 * (it.tr(step) - 1) + bank + 1)
                    for c in range(2):
                        for r in range(RT):
                            last = pe.transpose(tr[:, bank, c * N + r * P:c * N + (r + 1) * P],
                                                source[:, r, (2 * bank + c) * P:(2 * bank + c + 1) * P], id32[:])
                    last.then_inc(tr_ready, 1)

            def split_product(dst, pairs):
                for i, (s_hi, s_lo, m_hi, m_lo) in enumerate(pairs):
                    pe.matmul(dst, s_hi, m_hi, start=(i == 0), stop=False)
                    pe.matmul(dst, s_hi, m_lo, start=False, stop=False)
                    last = pe.matmul(dst, s_lo, m_hi, start=False, stop=(i == len(pairs) - 1))
                return last

            def take_pj(it, step):
                bank, use = it.pj(step)
                need(pe, pj_free, use - 1)
                return pj[:, bank, :]

            def rows_times_weight(it, step, r, t_hi, t_lo, m):
                dst = take_pj(it, step)
                rows = slice(r * P, (r + 1) * P)
                split_product(dst, [(t_hi[:, c, rows], t_lo[:, c, rows], w_hi[m][:, c, :], w_lo[m][:, c, :])
                                    for c in range(KC)]).then_inc(pj_ready, 1)

            def scores(it, u):
                n = it.n
                if u == 0:
                    need(pe, pj_free, it.pj_before)
                need(pe, exp_done, 4 * n + u)
                for j in range(2):
                    pe.matmul(lg[:, j, :], idbf[:], mask[it.parity][:].rearrange("p r n -> p (r n)"), start=True, stop=False)
                for r in range(RT):
                    for i, (qq, kk) in enumerate(((q_hi, k_hi), (q_hi, k_lo), (q_lo, k_hi))):
                        for j in range(2):
                            h = slice(DH * j, DH * (j + 1))
                            last = pe.matmul(lg[:, j, r * N:(r + 1) * N], qq[h, u, r * P:(r + 1) * P], kk[h, u, :],
                                             start=False, stop=(r == RT - 1 and i == 2))
                last.then_inc(lg_ready, 1)

            def transpose_probs(it, u):
                use = it.tr(f"PT{u}")
                need(pe, exp_done, 4 * it.n + u + 1)
                for j in range(2):
                    need(pe, tr_free, 2 * (use - 1) + j + 1)
                    for kt in range(RT):
                        for r in range(RT):
                            last = pe.transpose(tr[:, j, kt * N + r * P:kt * N + (r + 1) * P],
                                                p_exp[:, 2 * j + r, kt * P:(kt + 1) * P], id32[:])
                    last.then_inc(tr_ready, 1)

            def probs_times_v(it, u):
                n = it.n
                if u == 0:
                    need(pe, o_n_done, 2 * n)
                    need(pe, pj_free, it.pj("V1")[1] + 1)
                need(pe, tr_free, 2 * it.tr(f"PT{u}") + 2)
                for j in range(2):
                    h = slice((2 * u + j) * DH, (2 * u + j + 1) * DH)
                    for r in range(RT):
                        cols = [slice(kt * N + r * P, kt * N + (r + 1) * P) for kt in range(RT)]
                        last = split_product(o_ps[:, r, h], [(pt_hi[:, j, cols[kt]], pt_lo[:, j, cols[kt]],
                                                              v_hi[:, kt, h], v_lo[:, kt, h]) for kt in range(RT)])
                if u == NH // 2 - 1:
                    last.then_inc(o_ready, 1)

            def head_columns(it, step, m, half):
                dst = take_pj(it, step)
                for c2 in range(2):
                    cols = slice((2 * half + c2) * P, (2 * half + c2 + 1) * P)
                    last = split_product(dst[:, c2 * N:(c2 + 1) * N],
                                         [(w_hi[m][:, c, cols], w_lo[m][:, c, cols], ht_hi[1][:, c, :], ht_lo[1][:, c, :])
                                          for c in range(KC)])
                last.then_inc(pj_ready, 1)

            pe.wait_ge(ident_ready, 2)
            pe.wait_ge(w_lo_done, 5)
            pe.wait_ge(bv_lo_done, 1)
            split_product(lg[:, 0, :], [(bv_hi[:, c:c + 1].to_broadcast([P, P]), bv_lo[:, c:c + 1].to_broadcast([P, P]),
                                         w_hi["o"][:, c, :], w_lo["o"][:, c, :]) for c in range(KC)]).then_inc(out_bias_summed, 1)
            pe.wait_ge(out_bias_done, 1)
            pe.wait_ge(wa_lo_done, 1)

            def body(it):
                n = it.n
                a, c = n + 1, n
                if it.has("A"):
                    to_transposed("T0", it, hn[0], hn_done[0], 2 * (a + 1))
                if it.has("C"):
                    scores(it, 0)
                if it.has("A"):
                    need(pe, tr_free, 2 * it.tr("T0") + 2)
                    rows_times_weight(it, "WH0", 0, ht_hi[0], ht_lo[0], "gat")
                    rows_times_weight(it, "WH1", 1, ht_hi[0], ht_lo[0], "gat")
                    dst = take_pj(it, "S")
                    for r in range(RT):
                        rows = slice(r * P, (r + 1) * P)
                        last = split_product(dst[:, 2 * r:2 * r + 2],
                                             [(ht_hi[0][:, k, rows], ht_lo[0][:, k, rows], wa_hi[:, k, :], wa_lo[:, k, :])
                                              for k in range(KC)])
                    last.then_inc(pj_ready, 1)
                if it.has("C"):
                    transpose_probs(it, 0)
                    scores(it, 1)
                if it.has("A"):
                    dst = take_pj(it, "ZT")
                    need(pe, mask_done, a + 1)
                    need(pe, pj_free, it.pj("S")[1] + 1)
                    for jt in range(RT):
                        for r in range(RT):
                            part = dst[:, jt * N + r * P:jt * N + (r + 1) * P]
                            pe.matmul(part, mask[1 - it.parity][:, r, jt * P:(jt + 1) * P], idbf[:], start=True, stop=False)
                            pe.matmul(part, si_hi[:, r:r + 1].to_broadcast([P, P]), id16[:], start=False, stop=False)
                            last = pe.matmul(part, si_lo[:, r:r + 1].to_broadcast([P, P]), id16[:], start=False, stop=True)
                    last.then_inc(pj_ready, 1)
                if it.has("C"):
                    rows_times_weight(it, "V0", 0, ht_hi[1], ht_lo[1], "v")
                    rows_times_weight(it, "V1", 1, ht_hi[1], ht_lo[1], "v")
                    probs_times_v(it, 0)
                    transpose_probs(it, 1)
                    scores(it, 2)
                if it.has("A"):
                    need(pe, p0_lo_done, 2 * (a + 1))
                    for r in range(RT):
                        dst = take_pj(it, f"AT{r}")
                        rows = slice(r * P, (r + 1) * P)
                        split_product(dst, [(p0_hi[:, jt, rows], p0_lo[:, jt, rows], wh_hi[:, jt, :], wh_lo[:, jt, :])
                                            for jt in range(RT)]).then_inc(pj_ready, 1)
                if it.has("C"):
                    probs_times_v(it, 1)
                if it.has("W"):
                    need(pe, tr_free, 2 * it.tr_before)
                    rows_times_weight(it, "WO0", 0, ot_hi, ot_lo, "o")
                if it.has("C"):
                    transpose_probs(it, 2)
                    scores(it, 3)
                if it.has("W"):
                    rows_times_weight(it, "WO1", 1, ot_hi, ot_lo, "o")
                if it.has("A"):
                    to_transposed("T1", it, hn[1], hn_done[1], 2 * (a + 1))
                if it.has("C"):
                    probs_times_v(it, 2)
                    transpose_probs(it, 3)
                if it.has("A"):
                    need(pe, tr_free, 2 * it.tr("T1") + 2)
                    head_columns(it, "Q0", "q", 0)
                if it.has("C"):
                    probs_times_v(it, 3)
                if it.has("A"):
                    head_columns(it, "Q1", "q", 1)
                if it.has("C"):
                    to_transposed("OT", it, o_n, o_n_done, 2 * (c + 1))
                if it.has("A"):
                    head_columns(it, "K0", "k", 0)
                    head_columns(it, "K1", "k", 1)

            every_iteration(pe, body)

        @block.scalar
        def _(act):
            def split_tr(it, step, hi, func):
                for bank in range(2):
                    need(act, tr_ready, 2 * it.tr(step) + bank + 1)
                    act.activation(hi(bank), tr[:, bank, :], func).then_inc(tr_hi, 1)

            def normalise(ln, source, g):
                need(act, shift_done[ln], g + 1)
                for r in range(RT):
                    act.activation(hn[ln][:, r, :], source[:, r, :], ACT.Relu, bias=shift[ln][:, r:r + 1],
                                   scale=rstd[ln][:, r:r + 1]).then_inc(hn_done[ln], 1)

            def exps(it, u):
                need(act, max_scaled, 4 * it.n + u + 1)
                for j in range(2):
                    for r in range(RT):
                        last = act.activation(p_exp[:, 2 * j + r, :], lg[:, j, r * N:(r + 1) * N], ACT.Exp,
                                              bias=negmax_scaled[:, 2 * j + r:2 * j + r + 1], scale=SCORE,
                                              accum_out=p_sum[:, r, 2 * u + j:2 * u + j + 1])
                last.then_inc(exp_done, 1)

            def bank_of(it, step):
                bank, use = it.pj(step)
                need(act, pj_ready, use + 1)
                return pj[:, bank, :]

            for m in names:
                act.wait_ge(w_loaded[m], 16)
                act.activation(w_hi[m][:], w_raw[m][:], ACT.Copy, scale=WS).then_inc(w_hi_done, 1)
            act.wait_ge(wa_summed, 2 * KC)
            act.activation(wa_hi[:], wa[:], ACT.Copy).then_inc(wa_hi_done, 1)
            act.wait_ge(bias_scaled, 3)
            act.activation(bv_hi[:], bias["v"][:], ACT.Copy).then_inc(bv_hi_done, 1)

            def body(it):
                n = it.n
                a = n + 1
                if it.has("A"):
                    split_tr(it, "T0", lambda bank: ht_hi[0][:, 2 * bank:2 * bank + 2, :], ACT.Copy)
                if it.has("C"):
                    exps(it, 0)
                if it.has("A"):
                    for r in range(RT):
                        act.activation(wh_hi[:, r, :], bank_of(it, f"WH{r}"), ACT.Copy).then_inc(wh_hi_done, 1)
                    s = bank_of(it, "S")[:, 0:2 * RT].rearrange("p (r s) -> p r s", s=2)
                    act.activation(si_hi[:], s[:, :, 0], ACT.Copy).then_inc(s_hi_done, 1)
                    act.activation(sj_bias[:], s[:, :, 1], ACT.Copy, scale=(1 - LEAK) / WS).then_inc(s_hi_done, 1)
                if it.has("C"):
                    split_tr(it, "PT0", lambda j: pt_hi[:, j, :], ACT.Copy)
                if it.has("A"):
                    z = bank_of(it, "ZT")
                    need(act, s_hi_done, 2 * (a + 1))
                    for jt in range(RT):
                        last = act.activation(z_relu[:, jt, :], z[:, jt * N:(jt + 1) * N], ACT.Relu,
                                              bias=sj_bias[:, jt:jt + 1], scale=(1 - LEAK) / WS)
                    last.then_inc(z_relu_done, 1)
                if it.has("C"):
                    exps(it, 1)
                if it.has("A"):
                    need(act, z_max_done, a + 1)
                    for jt in range(RT):
                        last = act.activation(p0[:, jt, :], z_e[:, jt, :], ACT.Exp, bias=z_negmax[:, jt:jt + 1],
                                              accum_out=z_sum[:, jt:jt + 1])
                    last.then_inc(z_exp_done, 1)
                if it.has("C"):
                    act.activation(v_hi[:, 0, :], bank_of(it, "V0"), ACT.Copy).then_inc(v_hi_done, 1)
                if it.has("A"):
                    need(act, z_scale_done, a + 1)
                    need(act, z_exp_done, a + 1)
                    for jt in range(RT):
                        act.activation(p0_hi[:, jt, :], p0[:, jt, :], ACT.Copy, scale=z_inv16[:, jt:jt + 1]).then_inc(p0_hi_done, 1)
                if it.has("C"):
                    act.activation(v_hi[:, 1, :], bank_of(it, "V1"), ACT.Copy).then_inc(v_hi_done, 1)
                    split_tr(it, "PT1", lambda j: pt_hi[:, j, :], ACT.Copy)
                if it.has("A"):
                    for r in range(RT):
                        bank = bank_of(it, f"AT{r}")
                        need(act, x1_kept_done, 2 * a)
                        act.activation(relu_part[:, r, :], bank, ACT.Relu, scale=(1 - LEAK) / WS ** 2).then_inc(at_relu_done, 1)
                if it.has("C"):
                    exps(it, 2)
                    split_tr(it, "PT2", lambda j: pt_hi[:, j, :], ACT.Copy)
                if it.has("A"):
                    normalise(1, x1, a)
                if it.has("C"):
                    exps(it, 3)
                if it.has("A"):
                    split_tr(it, "T1", lambda bank: ht_hi[1][:, 2 * bank:2 * bank + 2, :], ACT.Copy)
                if it.has("C"):
                    split_tr(it, "PT3", lambda j: pt_hi[:, j, :], ACT.Copy)
                if it.has("A"):
                    head_chunks(it, "Q0", q_hi, "q", 0)
                    head_chunks(it, "Q1", q_hi, "q", 1)
                if it.has("N"):
                    if it.has("A"):
                        need(act, tr_ready, 2 * it.tr("T0") + 2)
                    normalise(0, x_in, n + 2)
                if it.has("C"):
                    split_tr(it, "OT", lambda bank: ot_hi[:, 2 * bank:2 * bank + 2, :], ACT.Copy)
                if it.has("A"):
                    head_chunks(it, "K0", k_hi, "k", 0)
                    head_chunks(it, "K1", k_hi, "k", 1)

            def head_chunks(it, step, hi, m, half):
                bank = bank_of(it, step)
                for c2 in range(2):
                    c = 2 * half + c2
                    last = act.activation(hi[:, c, :], bank[:, c2 * N:(c2 + 1) * N], ACT.Identity, bias=bias[m][:, c:c + 1])
                last.then_inc(qk_hi_done, 1)

            every_iteration(act, body)

        @block.vector
        def _(dve):
            def halves(t):
                return lambda bank: t[:, 2 * bank:2 * bank + 2, :].rearrange("p c n -> p (c n)")

            def split_tr(it, step, hi, lo):
                for bank in range(2):
                    need(dve, tr_hi, 2 * it.tr(step) + bank + 1)
                    dve.tensor_tensor(lo(bank), tr[:, bank, :], hi(bank), ALU.subtract).then_inc(tr_free, 1)

            def remainder(it, step, hi_done, value, hi, lo):
                bank, _ = it.pj(step)
                need(dve, hi_done, value)
                dve.tensor_tensor(lo, pj[:, bank, :], hi, ALU.subtract).then_inc(pj_free, 1)

            def maxima(it, u):
                need(dve, lg_ready, 4 * it.n + u + 1)
                need(dve, exp_done, 4 * it.n + u)
                dve.tensor_reduce(negmax[:], lg[:].rearrange("p j (r n) -> p (j r) n", r=RT), AX_X, ALU.max,
                                  negate=True).then_inc(max_done, 1)
                need(dve, max_done, 4 * it.n + u + 1)
                dve.tensor_scalar(negmax_scaled[:], negmax[:], SCORE, None, ALU.mult).then_inc(max_scaled, 1)

            def stats_of(ln, source, ready, values):
                for r in range(RT):
                    need(dve, ready, values[r])
                    dve.bn_stats(stats[ln][:, r, :], source[:, r, :]).then_inc(stats_done[ln], 1)

            def ln_terms_of(ln, g):
                for r in range(RT):
                    dve.bn_aggr(moments[ln][:, r, :], stats[ln][:, r, :]).then_inc(moments_done[ln], 1)
                need(dve, moments_done[ln], 2 * (g + 1))
                need(dve, shift_done[ln], g)
                dve.tensor_scalar(neg_mean[ln][:], moments[ln][:, :, 0], -1.0, None, ALU.mult).then_inc(ln_terms[ln], 1)
                dve.tensor_scalar(var_eps[ln][:], moments[ln][:, :, 1], EPS, None, ALU.add).then_inc(ln_terms[ln], 1)

            for i, m in enumerate(names):
                dve.wait_ge(w_hi_done, i + 1)
                dve.scalar_tensor_tensor(out=w_lo[m][:].rearrange("p c n -> p (c n)"), in0=w_raw[m][:].rearrange("p c n -> p (c n)"),
                                         scalar=WS, in1=w_hi[m][:].rearrange("p c n -> p (c n)"), op0=ALU.mult,
                                         op1=ALU.subtract).then_inc(w_lo_done, 1)
                if m == "gat":
                    dve.wait_ge(a_loaded, 16)
                    for c in range(KC):
                        for s in range(2):
                            if c:
                                dve.wait_ge(wa_summed, 2 * c)
                            dve.scalar_tensor_tensor(out=wa_prod[:, s, :], in0=w_raw[m][:, c, :], scalar=WS, in1=a_rows[:, s, :],
                                                     op0=ALU.mult, op1=ALU.mult, accum_out=wa[:, c, s:s + 1]).then_inc(wa_summed, 1)
            dve.wait_ge(wa_hi_done, 1)
            dve.tensor_tensor(wa_lo[:], wa[:], wa_hi[:], ALU.subtract).then_inc(wa_lo_done, 1)
            dve.wait_ge(bias_loaded, 64)
            for m in "qkv":
                dve.tensor_scalar(bias[m][:], bias_raw[m][:], WS, None, ALU.mult).then_inc(bias_scaled, 1)
            dve.wait_ge(bv_hi_done, 1)
            dve.tensor_tensor(bv_lo[:], bias["v"][:], bv_hi[:], ALU.subtract).then_inc(bv_lo_done, 1)
            dve.wait_ge(out_bias_summed, 1)
            dve.scalar_tensor_tensor(out=out_bias[:], in0=lg[:, 0, :], scalar=1 / WS ** 2, in1=bo_rows[:], op0=ALU.mult,
                                     op1=ALU.add).then_inc(out_bias_done, 1)
            dve.wait_ge(out_bias_done, 1)

            def body(it):
                n = it.n
                a, c, w, f = n + 1, n, n - 1, n + 2
                if it.has("A"):
                    split_tr(it, "T0", halves(ht_hi[0]), halves(ht_lo[0]))
                if it.has("C"):
                    maxima(it, 0)
                if it.has("A"):
                    for r in range(RT):
                        remainder(it, f"WH{r}", wh_hi_done, 2 * a + r + 1, wh_hi[:, r, :], wh_lo[:, r, :])
                    bank, _ = it.pj("S")
                    need(dve, s_hi_done, 2 * (a + 1))
                    s = pj[:, bank, 0:2 * RT].rearrange("p (r s) -> p r s", s=2)
                    dve.tensor_tensor(si_lo[:], s[:, :, 0], si_hi[:], ALU.subtract).then_inc(pj_free, 1)
                if it.has("C"):
                    split_tr(it, "PT0", lambda j: pt_hi[:, j, :], lambda j: pt_lo[:, j, :])
                    maxima(it, 1)
                if it.has("A"):
                    bank, _ = it.pj("ZT")
                    need(dve, z_relu_done, a + 1)
                    dve.scalar_tensor_tensor(out=z_e[:].rearrange("p r n -> p (r n)"), in0=pj[:, bank, :], scalar=LEAK / WS,
                                             in1=z_relu[:].rearrange("p r n -> p (r n)"), op0=ALU.mult, op1=ALU.add).then_inc(pj_free, 1)
                    need(dve, pj_free, it.pj("ZT")[1] + 1)
                    dve.tensor_reduce(z_negmax[:], z_e[:], AX_X, ALU.max, negate=True).then_inc(z_max_done, 1)
                if it.has("C"):
                    remainder(it, "V0", v_hi_done, 2 * c + 1, v_hi[:, 0, :], v_lo[:, 0, :])
                if it.has("A"):
                    need(dve, z_exp_done, a + 1)
                    dve.reciprocal(z_inv[:], z_sum[:]).then_inc(z_inv_done, 1)
                    need(dve, z_inv_done, a + 1)
                    dve.tensor_scalar(z_inv16[:], z_inv[:], WS, None, ALU.mult).then_inc(z_scale_done, 1)
                    need(dve, z_scale_done, a + 1)
                    for jt in range(RT):
                        need(dve, p0_hi_done, 2 * a + jt + 1)
                        dve.scalar_tensor_tensor(out=p0_lo[:, jt, :], in0=p0[:, jt, :], scalar=z_inv16[:, jt:jt + 1],
                                                 in1=p0_hi[:, jt, :], op0=ALU.mult, op1=ALU.subtract).then_inc(p0_lo_done, 1)
                if it.has("C"):
                    remainder(it, "V1", v_hi_done, 2 * c + 2, v_hi[:, 1, :], v_lo[:, 1, :])
                    split_tr(it, "PT1", lambda j: pt_hi[:, j, :], lambda j: pt_lo[:, j, :])
                    maxima(it, 2)
                if it.has("A"):
                    for r in range(RT):
                        bank, _ = it.pj(f"AT{r}")
                        need(dve, at_relu_done, 2 * a + r + 1)
                        dve.scalar_tensor_tensor(out=leak_part[:, r, :], in0=pj[:, bank, :], scalar=LEAK / WS ** 2,
                                                 in1=x_in[:, r, :], op0=ALU.mult, op1=ALU.add).then_inc(pj_free, 1)
                    stats_of(1, x1, x1_done, (2 * a + 1, 2 * a + 2))
                    need(dve, stats_done[1], 2 * (a + 1))

                def y_before_relu(r):
                    bank, use = it.pj(f"WO{r}")
                    need(dve, pj_ready, use + 1)
                    dve.scalar_tensor_tensor(out=y_lin[:, r, :], in0=pj[:, bank, :], scalar=1 / WS ** 2, in1=out_bias[:],
                                             op0=ALU.mult, op1=ALU.add).then_inc(pj_free, 1)

                def y_result(r):
                    need(dve, pj_free, it.pj(f"WO{r}")[1] + 1)
                    need(dve, y_stored, 16 * w)
                    need(dve, x1_kept_done, 2 * (w + 1))
                    dve.scalar_tensor_tensor(out=y_out[:, r, :], in0=y_lin[:, r, :], scalar=0.0,
                                             in1=x1_kept[1 - it.parity][:, r, :], op0=ALU.max, op1=ALU.add).then_inc(y_done, 1)

                if it.has("W"):
                    y_before_relu(0)
                if it.has("A"):
                    ln_terms_of(1, a)
                if it.has("W"):
                    y_result(0)
                if it.has("C"):
                    split_tr(it, "PT2", lambda j: pt_hi[:, j, :], lambda j: pt_lo[:, j, :])
                    maxima(it, 3)
                if it.has("W"):
                    y_before_relu(1)
                    y_result(1)
                if it.has("A"):
                    split_tr(it, "T1", halves(ht_hi[1]), halves(ht_lo[1]))
                if it.has("N"):
                    stats_of(0, x_in, x_loaded, (16 * (f + 1), 16 * (f + 1)))
                    need(dve, stats_done[0], 2 * (f + 1))
                    need(dve, adj_loaded, 16 * (f + 1))
                    dve.tensor_scalar(mask[it.parity][:], adj_in[:], 0.0, MASKED, ALU.is_le, ALU.mult).then_inc(mask_done, 1)
                    ln_terms_of(0, f)
                if it.has("C"):
                    split_tr(it, "PT3", lambda j: pt_hi[:, j, :], lambda j: pt_lo[:, j, :])
                if it.has("A"):
                    head_chunks(it, "Q0", q_hi, q_lo, "q", 0, 4 * a + 1)
                if it.has("A"):
                    head_chunks(it, "Q1", q_hi, q_lo, "q", 1, 4 * a + 2)
                if it.has("C"):
                    need(dve, exp_done, 4 * (c + 1))
                    dve.reciprocal(p_inv[:], p_sum[:]).then_inc(p_inv_done, 1)
                    need(dve, p_inv_done, c + 1)
                    need(dve, o_ready, c + 1)
                    for r in range(RT):
                        dve.tensor_tensor(o_n[:, r, :].rearrange("p (h d) -> p h d", h=NH),
                                          o_ps[:, r, :].rearrange("p (h d) -> p h d", h=NH),
                                          p_inv[:, r, :].unsqueeze(2).to_broadcast([P, NH, DH]), ALU.mult).then_inc(o_n_done, 1)
                    split_tr(it, "OT", halves(ot_hi), halves(ot_lo))
                if it.has("A"):
                    head_chunks(it, "K0", k_hi, k_lo, "k", 0, 4 * a + 3)
                    head_chunks(it, "K1", k_hi, k_lo, "k", 1, 4 * a + 4)

            def head_chunks(it, step, hi, lo, m, half, value):
                bank, _ = it.pj(step)
                need(dve, qk_hi_done, value)
                for c2 in range(2):
                    c = 2 * half + c2
                    last = dve.scalar_tensor_tensor(out=lo[:, c, :], in0=pj[:, bank, c2 * N:(c2 + 1) * N],
                                                    scalar=bias[m][:, c:c + 1], in1=hi[:, c, :], op0=ALU.add, op1=ALU.subtract)
                last.then_inc(pj_free, 1)

            every_iteration(dve, body)


_INS = ["x", "adj", "L0_gnn_W", "L0_gnn_a", "L1_gnn_Wq", "L1_gnn_bq", "L1_gnn_Wk", "L1_gnn_bk", "L1_gnn_Wv", "L1_gnn_bv",
        "L1_gnn_Wo", "L1_gnn_bo"]


def kernel(**inputs):
    import numpy as _np
    import concourse.bacc as _bacc
    from concourse import mybir as _mybir
    from concourse.bass_utils import run_bass_kernel_spmd as _run

    nc = _bacc.Bacc("TRN2", target_bir_lowering=False, num_devices=1)
    arrays, args = {}, []
    for name in _INS:
        a = _np.ascontiguousarray(inputs[name])
        arrays[f"in_{name}_dram"] = a
        args.append(nc.dram_tensor(f"in_{name}_dram", a.shape, _mybir.dt.from_np(a.dtype), kind="ExternalInput").ap())
    shape = arrays["in_x_dram"].shape
    args.append(nc.dram_tensor("out_0_dram", shape, _mybir.dt.float32, kind="ExternalOutput").ap())
    build(nc, *args)
    r = _run(nc, [arrays], core_ids=[0])
    return r.results[0]["out_0_dram"]
```

```python
from contextlib import ExitStack

import concourse.bass as bass
from concourse import mybir

F32 = mybir.dt.float32
F16 = mybir.dt.float16
BF16 = mybir.dt.bfloat16
I32 = mybir.dt.int32
ACT = mybir.ActivationFunctionType
ALU = mybir.AluOpType
AX_X = mybir.AxisListType.X

P = 128
NH = 8
EPS = 1e-5
LEAK = 0.2
MASKED = -1e30
NO_SCORE = -3e38
WS = 16.0

TR_STEPS = ["T0", "PT0", "PT1", "PT2", "T1", "PT3", "OT"]
PJ_STEPS = ["K1", "WH0", "WH1", "S", "ZT", "V0", "V1", "AT0", "AT1", "WO0", "WO1", "Q0", "Q1", "K0"]
STEP_OF = {"T0": "A", "T1": "A", "OT": "C", "WH0": "A", "WH1": "A", "S": "A", "ZT": "A", "V0": "C", "V1": "C",
           "AT0": "A", "AT1": "A", "WO0": "W", "WO1": "W", "Q0": "A", "Q1": "A", "K0": "A", "K1": "C",
           "PT0": "C", "PT1": "C", "PT2": "C", "PT3": "C"}


class Iteration:

    def __init__(self, n, parity, stages, graphs):
        self.n, self.parity, self.stages = n, parity, stages
        self.filling = "A" in stages and "C" not in stages
        self.tr_before, self.pj_before = self.uses_before(n, graphs)
        self.pj_parity = self.pj_before % 2 if isinstance(n, int) else 1

    @staticmethod
    def uses_before(n, graphs):
        if isinstance(n, int) and n < 1:
            return {-2: (0, 0), -1: (0, 0), 0: (2, 9)}[n]
        if isinstance(n, int) and n == graphs:
            return 2 + 7 * (n - 1) + 5, 14 * (n - 1) + 7 + 5
        return 2 + 7 * n, 14 * n + 7

    def has(self, stage):
        return stage in self.stages

    def tr(self, step):
        return self.tr_before + [s for s in TR_STEPS if self.has(STEP_OF[s])].index(step)

    def pj(self, step):
        at = [s for s in PJ_STEPS if self.has(STEP_OF[s])].index(step)
        return (self.pj_parity + at) % 2, self.pj_before + at


def need(eng, sem, value):
    if isinstance(value, int) and value <= 0:
        return
    eng.wait_ge(sem, value)


def build(nc, x, adj, w_gat, a_gat, wq, bq, wk, bk, wv, bv, wo, bo, out):
    B, N, D = x.shape
    KC = D // P
    RT = N // P
    DH = D // NH
    SCORE = float(DH) ** -0.5 / (WS * WS)
    assert (N, D, DH) == (256, 512, 64) and B >= 6 and B % 2 == 0

    with ExitStack() as ctx:
        def sb(name, shape, dt):
            return ctx.enter_context(nc.sbuf_tensor(name, shape, dt))

        def sem(name):
            return ctx.enter_context(nc.semaphore(name))

        tr = ctx.enter_context(nc.psum_tensor("tr", [P, 2, 512], F32))
        lg = ctx.enter_context(nc.psum_tensor("lg", [P, 2, 512], F32))
        pj = ctx.enter_context(nc.psum_tensor("pj", [P, 2, 512], F32))
        o_ps = ctx.enter_context(nc.psum_tensor("o_ps", [P, RT, 512], F32))

        id32 = sb("id32", [P, P], F32)
        id16 = sb("id16", [P, P], F16)
        idbf = sb("idbf", [P, P], BF16)
        neg_half = sb("neg_half", [P, RT], F32)
        names = ("gat", "q", "k", "v", "o")
        w_dram = dict(zip(names, (w_gat, wq, wk, wv, wo)))
        w_raw = {m: sb(f"w_raw_{m}", [P, KC, D], F32) for m in names}
        w_hi = {m: sb(f"w_hi_{m}", [P, KC, D], F16) for m in names}
        w_lo = {m: sb(f"w_lo_{m}", [P, KC, D], F16) for m in names}
        a_rows = sb("a_rows", [P, 2, D], F32)
        wa = sb("wa", [P, KC, 2], F32)
        wa_hi = sb("wa_hi", [P, KC, 2], F16)
        wa_lo = sb("wa_lo", [P, KC, 2], F16)
        wa_prod = sb("wa_prod", [P, 2, D], F32)
        bias_raw = {m: sb(f"bias_raw_{m}", [P, KC], F32) for m in "qkv"}
        bias = {m: sb(f"bias_{m}", [P, KC], F32) for m in "qkv"}
        bv_hi = sb("bv_hi", [P, KC], F16)
        bv_lo = sb("bv_lo", [P, KC], F16)
        bo_rows = sb("bo_rows", [P, D], F32)
        out_bias = sb("out_bias", [P, D], F32)

        x_in = sb("x_in", [P, RT, D], F32)
        adj_in = sb("adj_in", [P, RT, N], I32)
        mask = [sb(f"mask{i}", [P, RT, N], BF16) for i in range(2)]
        stats = [sb(f"stats{i}", [P, RT, 6], F32) for i in range(2)]
        moments = [sb(f"moments{i}", [P, RT, 2], F32) for i in range(2)]
        neg_mean = [sb(f"neg_mean{i}", [P, RT], F32) for i in range(2)]
        var_eps = [sb(f"var_eps{i}", [P, RT], F32) for i in range(2)]
        shift = [sb(f"shift{i}", [P, RT], F32) for i in range(2)]
        rstd = [sb(f"rstd{i}", [P, RT], F32) for i in range(2)]
        hn = [sb(f"hn{i}", [P, RT, D], F32) for i in range(2)]
        ht_hi = [sb(f"ht_hi{i}", [P, KC, N], F16) for i in range(2)]
        ht_lo = [sb(f"ht_lo{i}", [P, KC, N], F16) for i in range(2)]

        wh_hi = sb("wh_hi", [P, RT, D], F16)
        wh_lo = sb("wh_lo", [P, RT, D], F16)
        si_hi = sb("si_hi", [P, RT], F16)
        si_lo = sb("si_lo", [P, RT], F16)
        sj_bias = sb("sj_bias", [P, RT], F32)
        z_relu = sb("z_relu", [P, RT, N], F32)
        z_e = sb("z_e", [P, RT, N], F32)
        z_negmax = sb("z_negmax", [P, RT], F32)
        z_sum = sb("z_sum", [P, RT], F32)
        z_inv = sb("z_inv", [P, RT], F32)
        z_inv16 = sb("z_inv16", [P, RT], F32)
        p0 = sb("p0", [P, RT, N], F32)
        p0_hi = sb("p0_hi", [P, RT, N], F16)
        p0_lo = sb("p0_lo", [P, RT, N], F16)
        relu_part = sb("relu_part", [P, RT, D], F32)
        leak_part = sb("leak_part", [P, RT, D], F32)
        x1 = sb("x1", [P, RT, D], F32)
        x1_kept = [sb(f"x1_kept{i}", [P, RT, D], F32) for i in range(2)]

        q_hi = sb("q_hi", [P, KC, N], F16)
        q_lo = sb("q_lo", [P, KC, N], F16)
        k_hi = sb("k_hi", [P, KC, N], F16)
        k_lo = sb("k_lo", [P, KC, N], F16)
        v_hi = sb("v_hi", [P, RT, D], F16)
        v_lo = sb("v_lo", [P, RT, D], F16)
        negmax = sb("negmax", [P, 4], F32)
        scores_neg = sb("scores_neg", [P, 4, N], F32)
        wait_carrier = sb("wait_carrier", [P, 2], F32)
        p_exp = sb("p_exp", [P, 4, N], F32)
        p_sum = sb("p_sum", [P, RT, NH], F32)
        p_inv = sb("p_inv", [P, RT, NH], F32)
        pt_hi = [sb(f"pt_hi{i}", [P, 2, 512], F16) for i in range(2)]
        pt_lo = [sb(f"pt_lo{i}", [P, 2, 512], F16) for i in range(2)]
        o_n = sb("o_n", [P, RT, D], F32)
        ot_hi = sb("ot_hi", [P, KC, N], F16)
        ot_lo = sb("ot_lo", [P, KC, N], F16)
        y_lin = sb("y_lin", [P, RT, D], F32)
        y_out = sb("y_out", [P, RT, D], F32)

        ident_zeroed = sem("ident_zeroed")
        ident_ready = sem("ident_ready")
        w_loaded = {m: sem(f"w_loaded_{m}") for m in names}
        a_loaded = sem("a_loaded")
        bias_loaded = sem("bias_loaded")
        w_hi_done = sem("w_hi_done")
        w_lo_done = sem("w_lo_done")
        wa_summed = sem("wa_summed")
        wa_hi_done = sem("wa_hi_done")
        wa_lo_done = sem("wa_lo_done")
        bias_scaled = sem("bias_scaled")
        bv_hi_done = sem("bv_hi_done")
        bv_lo_done = sem("bv_lo_done")
        out_bias_summed = sem("out_bias_summed")
        out_bias_done = sem("out_bias_done")
        x_loaded = sem("x_loaded")
        adj_loaded = sem("adj_loaded")
        mask_done = sem("mask_done")
        stats_done = [sem(f"stats_done{i}") for i in range(2)]
        moments_done = [sem(f"moments_done{i}") for i in range(2)]
        ln_terms = [sem(f"ln_terms{i}") for i in range(2)]
        rstd_done = [sem(f"rstd_done{i}") for i in range(2)]
        shift_done = [sem(f"shift_done{i}") for i in range(2)]
        hn_done = [sem(f"hn_done{i}") for i in range(2)]
        tr_ready, tr_hi, tr_free = sem("tr_ready"), sem("tr_hi"), sem("tr_free")
        pj_ready, pj_free = sem("pj_ready"), sem("pj_free")
        wh_hi_done = sem("wh_hi_done")
        s_hi_done = sem("s_hi_done")
        z_relu_done = sem("z_relu_done")
        z_e_done = sem("z_e_done")
        z_max_done = sem("z_max_done")
        z_exp_done = sem("z_exp_done")
        z_inv_done = sem("z_inv_done")
        z_scale_done = sem("z_scale_done")
        p0_hi_done = sem("p0_hi_done")
        p0_lo_done = sem("p0_lo_done")
        at_relu_done = sem("at_relu_done")
        x1_done = sem("x1_done")
        x1_kept_done = sem("x1_kept_done")
        qk_hi_done = sem("qk_hi_done")
        v_hi_done = sem("v_hi_done")
        lg_ready = sem("lg_ready")
        masked_done = sem("masked_done")
        exp_done = sem("exp_done")
        o_ready = sem("o_ready")
        p_inv_done = sem("p_inv_done")
        o_n_done = sem("o_n_done")
        y_lin_done = sem("y_lin_done")
        y_done = sem("y_done")
        y_stored = sem("y_stored")

        x_rows = x.rearrange("b (r p) d -> b p r d", p=P)
        adj_rows = adj.rearrange("b (r p) n -> b p r n", p=P)
        out_rows = out.rearrange("b (r p) d -> b p r d", p=P)

        def every_iteration(eng, body, before=None):
            for n, stages in ((-2, "N"), (-1, "AN"), (0, "ACN")):
                if before and n in before:
                    before[n]()
                body(Iteration(n, n % 2, stages, B))
            last = B - 4
            with eng.Fori(1, last + 1, 2) as i:
                for step in range(2):
                    body(Iteration(i + step, (1 + step) % 2, "ACWN", B))
            for n, stages in ((last + 1, "ACWN"), (last + 2, "ACW"), (last + 3, "CW"), (last + 4, "W")):
                body(Iteration(n, n % 2, stages, B))

        block = ctx.enter_context(nc.Block())

        @block.sync
        def _(sp):
            sp.dma_start(x_in[:], x_rows[0]).then_inc(x_loaded, 16)
            sp.dma_start(adj_in[:], adj_rows[0]).then_inc(adj_loaded, 16)
            sp.dma_start(w_raw["gat"][:], w_dram["gat"].rearrange("(c p) n -> p c n", p=P)).then_inc(w_loaded["gat"], 16)
            a_bcast = a_gat.rearrange("(s d) one -> one s d", s=2).to_broadcast([P, 2, D])
            sp.dma_start(a_rows[:], a_bcast).then_inc(a_loaded, 16)
            for m in ("q", "k", "v", "o"):
                sp.dma_start(w_raw[m][:], w_dram[m].rearrange("(c p) n -> p c n", p=P)).then_inc(w_loaded[m], 16)
            with nc.allow_non_contiguous_dma(reason="three bias vectors, once"):
                for m, b in (("q", bq), ("k", bk), ("v", bv)):
                    sp.dma_start(bias_raw[m][:], b.rearrange("(c p) -> p c", p=P)).then_inc(bias_loaded, 16)
            sp.dma_start(bo_rows[:], bo.rearrange("(one d) -> one d", one=1).to_broadcast([P, D])).then_inc(bias_loaded, 16)

            def body(it):
                n = it.n
                f, w = n + 2, n - 1
                if it.has("N") and it.has("A"):
                    need(sp, mask_done, f)
                    sp.dma_start(adj_in[:], adj_rows[bass.ds(f, 1)].rearrange("b p r n -> p (b r) n")).then_inc(adj_loaded, 16)
                    need(sp, pj_free, it.pj("AT1")[1] + 1)
                    sp.dma_start(x_in[:], x_rows[bass.ds(f, 1)].rearrange("b p r d -> p (b r) d")).then_inc(x_loaded, 16)
                if it.has("W"):
                    need(sp, y_done, 2 * (w + 1))
                    sp.dma_start(out_rows[bass.ds(w, 1)].rearrange("b p r d -> p (b r) d"), y_out[:]).then_inc(y_stored, 16)

            every_iteration(sp, body)
            sp.wait_ge(y_stored, 16 * B)

        @block.gpsimd
        def _(pool):
            pool.memset(id32[:], 0.0).then_inc(ident_zeroed, 1)
            pool.memset(neg_half[:], -0.5).then_inc(ident_zeroed, 1)
            pool.wait_ge(ident_zeroed, 2)
            pool.affine_select(out=id32[:], in_=id32[:], compare_op=ALU.not_equal, fill=1.0, base=0,
                               pattern=[[-1, P]], channel_multiplier=1).then_inc(ident_zeroed, 1)
            pool.wait_ge(ident_zeroed, 3)
            pool.tensor_copy(id16[:], id32[:]).then_inc(ident_ready, 1)
            pool.tensor_copy(idbf[:], id32[:]).then_inc(ident_ready, 1)

            def norm_factors(ln, g):
                need(pool, ln_terms[ln], 2 * (g + 1))
                pool.tensor_tensor(rstd[ln][:], var_eps[ln][:], neg_half[:], ALU.pow).then_inc(rstd_done[ln], 1)
                need(pool, rstd_done[ln], g + 1)
                pool.tensor_tensor(shift[ln][:], neg_mean[ln][:], rstd[ln][:], ALU.mult).then_inc(shift_done[ln], 1)

            def body(it):
                n = it.n
                a, f, w = n + 1, n + 2, n - 1
                if it.has("A"):
                    for r in range(RT):
                        need(pool, pj_free, it.pj(f"AT{r}")[1] + 1)
                        need(pool, hn_done[1], 2 * a)
                        pool.tensor_tensor(x1[:, r, :], relu_part[:, r, :], leak_part[:, r, :], ALU.add).then_inc(x1_done, 1)
                    norm_factors(1, a)
                    if it.has("W"):
                        need(pool, y_done, 2 * (w + 1))
                    for r in range(RT):
                        pool.tensor_tensor(x1_kept[1 - it.parity][:, r, :], relu_part[:, r, :], leak_part[:, r, :],
                                           ALU.add).then_inc(x1_kept_done, 1)
                if it.has("N"):
                    norm_factors(0, f)

            every_iteration(pool, body)

        @block.tensor
        def _(pe):
            def to_transposed(step, it, source, ready, value):
                need(pe, ready, value)
                for bank in range(2):
                    need(pe, tr_free, 2 * (it.tr(step) - 1) + bank + 1)
                    for c in range(2):
                        for r in range(RT):
                            last = pe.transpose(tr[:, bank, c * N + r * P:c * N + (r + 1) * P],
                                                source[:, r, (2 * bank + c) * P:(2 * bank + c + 1) * P], id32[:])
                    last.then_inc(tr_ready, 1)

            def split_product(dst, pairs, first=True, final=True):
                for i, (s_hi, s_lo, m_hi, m_lo) in enumerate(pairs):
                    pe.matmul(dst, s_hi, m_hi, start=(first and i == 0), stop=False)
                    pe.matmul(dst, s_hi, m_lo, start=False, stop=False)
                    last = pe.matmul(dst, s_lo, m_hi, start=False, stop=(final and i == len(pairs) - 1))
                return last

            def take_pj(it, step):
                bank, use = it.pj(step)
                need(pe, pj_free, use - 1)
                return pj[:, bank, :]

            def rows_times_weight(it, step, r, t_hi, t_lo, m, chunks=range(KC)):
                first, final = chunks[0] == 0, chunks[-1] == KC - 1
                dst = take_pj(it, step) if first else pj[:, it.pj(step)[0], :]
                rows = slice(r * P, (r + 1) * P)
                last = split_product(dst, [(t_hi[:, c, rows], t_lo[:, c, rows], w_hi[m][:, c, :], w_lo[m][:, c, :])
                                           for c in chunks], first, final)
                if final:
                    last.then_inc(pj_ready, 1)

            def scores(it, u):
                n = it.n
                if u == 0:
                    need(pe, pj_free, it.pj_before)
                if u == 2:
                    need(pe, pj_free, it.pj("K1")[1] + 1)
                need(pe, masked_done, 4 * n + u)
                for r in range(RT):
                    for i, (qq, kk) in enumerate(((q_hi, k_hi), (q_hi, k_lo), (q_lo, k_hi))):
                        for j in range(2):
                            h = slice(DH * j, DH * (j + 1))
                            last = pe.matmul(lg[:, j, r * N:(r + 1) * N], qq[h, u, r * P:(r + 1) * P], kk[h, u, :],
                                             start=(i == 0), stop=(i == 2))
                last.then_inc(lg_ready, 1)

            def transpose_probs(it, u):
                use = it.tr(f"PT{u}")
                need(pe, exp_done, 4 * it.n + u + 1)
                for j in range(2):
                    need(pe, tr_free, 2 * (use - 1) + j + 1)
                    for kt in range(RT):
                        for r in range(RT):
                            last = pe.transpose(tr[:, j, kt * N + r * P:kt * N + (r + 1) * P],
                                                p_exp[:, 2 * j + r, kt * P:(kt + 1) * P], id32[:])
                    last.then_inc(tr_ready, 1)

            def probs_times_v(it, u):
                n = it.n
                if u == 0:
                    need(pe, o_n_done, 2 * n)
                    need(pe, pj_free, it.pj("V1")[1] + 1)
                need(pe, tr_free, 2 * it.tr(f"PT{u}") + 2)
                for j in range(2):
                    h = slice((2 * u + j) * DH, (2 * u + j + 1) * DH)
                    for r in range(RT):
                        cols = [slice(kt * N + r * P, kt * N + (r + 1) * P) for kt in range(RT)]
                        last = split_product(o_ps[:, r, h], [(pt_hi[u % 2][:, j, cols[kt]], pt_lo[u % 2][:, j, cols[kt]],
                                                              v_hi[:, kt, h], v_lo[:, kt, h]) for kt in range(RT)])
                if u == NH // 2 - 1:
                    last.then_inc(o_ready, 1)

            def head_columns(it, step, m, half):
                dst = take_pj(it, step)
                for c2 in range(2):
                    cols = slice((2 * half + c2) * P, (2 * half + c2 + 1) * P)
                    last = split_product(dst[:, c2 * N:(c2 + 1) * N],
                                         [(w_hi[m][:, c, cols], w_lo[m][:, c, cols], ht_hi[1][:, c, :], ht_lo[1][:, c, :])
                                          for c in range(KC)])
                last.then_inc(pj_ready, 1)

            def set_up_gat():
                pe.wait_ge(ident_ready, 2)
                pe.wait_ge(w_lo_done, 1)
                pe.wait_ge(wa_lo_done, 1)

            def set_up_out_bias():
                pe.wait_ge(w_lo_done, 5)
                pe.wait_ge(bv_lo_done, 1)
                bv_pairs = [(b[:, c:c + 1].to_broadcast([P, P])) for c in range(KC) for b in (bv_hi, bv_lo)]
                split_product(lg[:, 0, :], [(bv_pairs[2 * c], bv_pairs[2 * c + 1], w_hi["o"][:, c, :], w_lo["o"][:, c, :])
                                            for c in range(KC)]).then_inc(out_bias_summed, 1)
                pe.wait_ge(out_bias_done, 1)

            def body(it):
                n = it.n
                a, c = n + 1, n
                if it.has("A"):
                    to_transposed("T0", it, hn[0], hn_done[0], 2 * (a + 1))
                if it.has("C"):
                    head_columns(it, "K1", "k", 1)
                    scores(it, 0)
                if it.has("A"):
                    need(pe, tr_free, 2 * it.tr("T0") + 2)
                    rows_times_weight(it, "WH0", 0, ht_hi[0], ht_lo[0], "gat")
                    rows_times_weight(it, "WH1", 1, ht_hi[0], ht_lo[0], "gat")
                    dst = take_pj(it, "S")
                    for r in range(RT):
                        rows = slice(r * P, (r + 1) * P)
                        last = split_product(dst[:, 2 * r:2 * r + 2],
                                             [(ht_hi[0][:, k, rows], ht_lo[0][:, k, rows], wa_hi[:, k, :], wa_lo[:, k, :])
                                              for k in range(KC)])
                    last.then_inc(pj_ready, 1)
                if it.has("C"):
                    transpose_probs(it, 0)
                    scores(it, 1)
                if it.has("A"):
                    dst = take_pj(it, "ZT")
                    need(pe, mask_done, a + 1)
                    need(pe, pj_free, it.pj("S")[1] + 1)
                    for jt in range(RT):
                        for r in range(RT):
                            part = dst[:, jt * N + r * P:jt * N + (r + 1) * P]
                            pe.matmul(part, mask[1 - it.parity][:, r, jt * P:(jt + 1) * P], idbf[:], start=True, stop=False)
                            pe.matmul(part, si_hi[:, r:r + 1].to_broadcast([P, P]), id16[:], start=False, stop=False)
                            last = pe.matmul(part, si_lo[:, r:r + 1].to_broadcast([P, P]), id16[:], start=False, stop=True)
                    last.then_inc(pj_ready, 1)
                if it.has("C"):
                    rows_times_weight(it, "V0", 0, ht_hi[1], ht_lo[1], "v")
                    rows_times_weight(it, "V1", 1, ht_hi[1], ht_lo[1], "v")
                    transpose_probs(it, 1)
                if it.has("A"):
                    need(pe, p0_lo_done, 2 * (a + 1))
                    for r in range(RT):
                        dst = take_pj(it, f"AT{r}")
                        rows = slice(r * P, (r + 1) * P)
                        split_product(dst, [(p0_hi[:, jt, rows], p0_lo[:, jt, rows], wh_hi[:, jt, :], wh_lo[:, jt, :])
                                            for jt in range(RT)]).then_inc(pj_ready, 1)
                if it.has("C"):
                    scores(it, 2)
                    probs_times_v(it, 0)
                    probs_times_v(it, 1)
                if it.has("W"):
                    need(pe, tr_free, 2 * it.tr_before)
                    rows_times_weight(it, "WO0", 0, ot_hi, ot_lo, "o")
                if it.has("C"):
                    transpose_probs(it, 2)
                    scores(it, 3)
                if it.has("W"):
                    rows_times_weight(it, "WO1", 1, ot_hi, ot_lo, "o", range(0, 1))
                if it.has("A"):
                    to_transposed("T1", it, hn[1], hn_done[1], 2 * (a + 1))
                if it.has("W"):
                    rows_times_weight(it, "WO1", 1, ot_hi, ot_lo, "o", range(1, KC))
                if it.has("C"):
                    probs_times_v(it, 2)
                    transpose_probs(it, 3)
                if it.has("A"):
                    if it.filling:
                        pe.wait_ge(w_lo_done, 3)
                    need(pe, tr_free, 2 * it.tr("T1") + 2)
                    head_columns(it, "Q0", "q", 0)
                if it.has("C"):
                    probs_times_v(it, 3)
                if it.has("A"):
                    head_columns(it, "Q1", "q", 1)
                if it.has("C"):
                    to_transposed("OT", it, o_n, o_n_done, 2 * (c + 1))
                if it.has("A"):
                    head_columns(it, "K0", "k", 0)

            every_iteration(pe, body, {-1: set_up_gat, 0: set_up_out_bias})

        @block.scalar
        def _(act):
            def split_tr(it, step, hi, func):
                for bank in range(2):
                    need(act, tr_ready, 2 * it.tr(step) + bank + 1)
                    act.activation(hi(bank), tr[:, bank, :], func).then_inc(tr_hi, 1)

            def split_probs(it, u):
                split_tr(it, f"PT{u}", lambda j: pt_hi[u % 2][:, j, :], ACT.Copy)

            def normalise(ln, source, g):
                need(act, shift_done[ln], g + 1)
                for r in range(RT):
                    act.activation(hn[ln][:, r, :], source[:, r, :], ACT.Relu, bias=shift[ln][:, r:r + 1],
                                   scale=rstd[ln][:, r:r + 1]).then_inc(hn_done[ln], 1)

            def exps(it, u):
                need(act, masked_done, 4 * it.n + u + 1)
                for j in range(2):
                    for r in range(RT):
                        last = act.activation(p_exp[:, 2 * j + r, :], scores_neg[:, 2 * j + r, :], ACT.Exp,
                                              bias=negmax[:, 2 * j + r:2 * j + r + 1], scale=-1.0,
                                              accum_out=p_sum[:, r, 2 * u + j:2 * u + j + 1])
                last.then_inc(exp_done, 1)

            def bank_of(it, step):
                bank, use = it.pj(step)
                need(act, pj_ready, use + 1)
                return pj[:, bank, :]

            def weight_heads(*which):
                for m in which:
                    act.wait_ge(w_loaded[m], 16)
                    act.activation(w_hi[m][:], w_raw[m][:], ACT.Copy, scale=WS).then_inc(w_hi_done, 1)

            def wa_head():
                act.wait_ge(wa_summed, 2 * KC)
                act.activation(wa_hi[:], wa[:], ACT.Copy).then_inc(wa_hi_done, 1)

            def bv_head():
                act.wait_ge(bias_scaled, 3)
                act.activation(bv_hi[:], bias["v"][:], ACT.Copy).then_inc(bv_hi_done, 1)

            def body(it):
                n = it.n
                a = n + 1
                if it.has("A"):
                    split_tr(it, "T0", lambda bank: ht_hi[0][:, 2 * bank:2 * bank + 2, :], ACT.Copy)
                if it.has("C"):
                    head_chunks(it, "K1", k_hi, "k", 1)
                    exps(it, 0)
                if it.has("A"):
                    for r in range(RT):
                        act.activation(wh_hi[:, r, :], bank_of(it, f"WH{r}"), ACT.Copy).then_inc(wh_hi_done, 1)
                    s = bank_of(it, "S")[:, 0:2 * RT].rearrange("p (r s) -> p r s", s=2)
                    act.activation(si_hi[:], s[:, :, 0], ACT.Copy).then_inc(s_hi_done, 1)
                    act.activation(sj_bias[:], s[:, :, 1], ACT.Copy, scale=(1 - LEAK) / WS).then_inc(s_hi_done, 1)
                if it.has("C"):
                    split_probs(it, 0)
                if it.has("A"):
                    z = bank_of(it, "ZT")
                    need(act, s_hi_done, 2 * (a + 1))
                    for jt in range(RT):
                        last = act.activation(z_relu[:, jt, :], z[:, jt * N:(jt + 1) * N], ACT.Relu,
                                              bias=sj_bias[:, jt:jt + 1], scale=(1 - LEAK) / WS)
                    last.then_inc(z_relu_done, 1)
                if it.has("C"):
                    exps(it, 1)
                if it.has("A"):
                    need(act, z_max_done, a + 1)
                    for jt in range(RT):
                        last = act.activation(p0[:, jt, :], z_e[:, jt, :], ACT.Exp, bias=z_negmax[:, jt:jt + 1],
                                              accum_out=z_sum[:, jt:jt + 1])
                    last.then_inc(z_exp_done, 1)
                if it.has("C"):
                    act.activation(v_hi[:, 0, :], bank_of(it, "V0"), ACT.Copy).then_inc(v_hi_done, 1)
                if it.has("A"):
                    need(act, z_scale_done, a + 1)
                    need(act, z_exp_done, a + 1)
                    for jt in range(RT):
                        act.activation(p0_hi[:, jt, :], p0[:, jt, :], ACT.Copy, scale=z_inv16[:, jt:jt + 1]).then_inc(p0_hi_done, 1)
                if it.filling:
                    weight_heads("q", "k")
                if it.has("C"):
                    act.activation(v_hi[:, 1, :], bank_of(it, "V1"), ACT.Copy).then_inc(v_hi_done, 1)
                    split_probs(it, 1)
                if it.has("A"):
                    for r in range(RT):
                        bank = bank_of(it, f"AT{r}")
                        need(act, x1_kept_done, 2 * a)
                        act.activation(relu_part[:, r, :], bank, ACT.Relu, scale=(1 - LEAK) / WS ** 2).then_inc(at_relu_done, 1)
                if it.filling:
                    weight_heads("v", "o")
                if it.has("C"):
                    exps(it, 2)
                if it.has("C"):
                    split_probs(it, 2)
                if it.has("A"):
                    normalise(1, x1, a)
                if it.has("A"):
                    split_tr(it, "T1", lambda bank: ht_hi[1][:, 2 * bank:2 * bank + 2, :], ACT.Copy)
                if it.has("C"):
                    exps(it, 3)
                    split_probs(it, 3)
                if it.has("A"):
                    head_chunks(it, "Q0", q_hi, "q", 0)
                if it.has("N"):
                    if it.has("A"):
                        need(act, tr_ready, 2 * it.tr("T0") + 2)
                    normalise(0, x_in, n + 2)
                if it.has("A"):
                    head_chunks(it, "Q1", q_hi, "q", 1)
                if it.has("C"):
                    split_tr(it, "OT", lambda bank: ot_hi[:, 2 * bank:2 * bank + 2, :], ACT.Copy)
                if it.has("A"):
                    head_chunks(it, "K0", k_hi, "k", 0)

            def head_chunks(it, step, hi, m, half):
                bank = bank_of(it, step)
                for c2 in range(2):
                    c = 2 * half + c2
                    last = act.activation(hi[:, c, :], bank[:, c2 * N:(c2 + 1) * N], ACT.Identity, bias=bias[m][:, c:c + 1])
                last.then_inc(qk_hi_done, 1)

            every_iteration(act, body, {-2: lambda: weight_heads("gat"), -1: wa_head, 0: bv_head})

        @block.vector
        def _(dve):
            def carry_wait(cell, sem, value):
                need(dve, sem, value)
                dve.memset(wait_carrier[:, cell:cell + 1], 0.0)

            def halves(t):
                return lambda bank: t[:, 2 * bank:2 * bank + 2, :].rearrange("p c n -> p (c n)")

            def split_tr(it, step, hi, lo):
                for bank in range(2):
                    need(dve, tr_hi, 2 * it.tr(step) + bank + 1)
                    dve.tensor_tensor(lo(bank), tr[:, bank, :], hi(bank), ALU.subtract).then_inc(tr_free, 1)

            def split_probs(it, u):
                split_tr(it, f"PT{u}", lambda j: pt_hi[u % 2][:, j, :], lambda j: pt_lo[u % 2][:, j, :])

            def remainder(it, step, hi_done, value, hi, lo):
                bank, _ = it.pj(step)
                need(dve, hi_done, value)
                dve.tensor_tensor(lo, pj[:, bank, :], hi, ALU.subtract).then_inc(pj_free, 1)

            def masked_scores(it, u):
                need(dve, lg_ready, 4 * it.n + u + 1)
                carry_wait(0, exp_done, 4 * it.n + u)
                for j in range(2):
                    for r in range(RT):
                        last = dve.tensor_tensor_reduce(out=scores_neg[:, 2 * j + r, :], in0=lg[:, j, r * N:(r + 1) * N],
                                                        in1=mask[it.parity][:, r, :], scale=-SCORE, scalar=-NO_SCORE,
                                                        op0=ALU.add, op1=ALU.min, accum_out=negmax[:, 2 * j + r:2 * j + r + 1])
                last.then_inc(masked_done, 1)

            def stats_of(ln, source, ready, values):
                for r in range(RT):
                    need(dve, ready, values[r])
                    dve.bn_stats(stats[ln][:, r, :], source[:, r, :]).then_inc(stats_done[ln], 1)

            def ln_terms_of(ln, g):
                for r in range(RT):
                    dve.bn_aggr(moments[ln][:, r, :], stats[ln][:, r, :]).then_inc(moments_done[ln], 1)
                need(dve, moments_done[ln], 2 * (g + 1))
                need(dve, shift_done[ln], g)
                dve.tensor_scalar(neg_mean[ln][:], moments[ln][:, :, 0], -1.0, None, ALU.mult).then_inc(ln_terms[ln], 1)
                dve.tensor_scalar(var_eps[ln][:], moments[ln][:, :, 1], EPS, None, ALU.add).then_inc(ln_terms[ln], 1)

            def weight_remainders(*which):
                for m in which:
                    dve.wait_ge(w_hi_done, names.index(m) + 1)
                    dve.scalar_tensor_tensor(out=w_lo[m][:].rearrange("p c n -> p (c n)"),
                                             in0=w_raw[m][:].rearrange("p c n -> p (c n)"), scalar=WS,
                                             in1=w_hi[m][:].rearrange("p c n -> p (c n)"), op0=ALU.mult,
                                             op1=ALU.subtract).then_inc(w_lo_done, 1)

            def set_up_first():
                dve.wait_ge(w_loaded["gat"], 16)
                dve.wait_ge(a_loaded, 16)
                for c in range(KC):
                    for s in range(2):
                        if c:
                            dve.wait_ge(wa_summed, 2 * (c - 1) + s + 1)
                        dve.scalar_tensor_tensor(out=wa_prod[:, s, :], in0=w_raw["gat"][:, c, :], scalar=WS, in1=a_rows[:, s, :],
                                                 op0=ALU.mult, op1=ALU.mult, accum_out=wa[:, c, s:s + 1]).then_inc(wa_summed, 1)
                dve.wait_ge(wa_hi_done, 1)
                dve.tensor_tensor(wa_lo[:], wa[:], wa_hi[:], ALU.subtract).then_inc(wa_lo_done, 1)
                weight_remainders("gat")

            def scale_biases():
                dve.wait_ge(bias_loaded, 64)
                for m in "qkv":
                    dve.tensor_scalar(bias[m][:], bias_raw[m][:], WS, None, ALU.mult).then_inc(bias_scaled, 1)

            def set_up_out_bias():
                dve.wait_ge(bv_hi_done, 1)
                dve.tensor_tensor(bv_lo[:], bias["v"][:], bv_hi[:], ALU.subtract).then_inc(bv_lo_done, 1)
                dve.wait_ge(out_bias_summed, 1)
                dve.scalar_tensor_tensor(out=out_bias[:], in0=lg[:, 0, :], scalar=1 / WS ** 2, in1=bo_rows[:], op0=ALU.mult,
                                         op1=ALU.add).then_inc(out_bias_done, 1)

            def body(it):
                n = it.n
                a, c, w, f = n + 1, n, n - 1, n + 2
                if it.has("A"):
                    split_tr(it, "T0", halves(ht_hi[0]), halves(ht_lo[0]))
                if it.has("C"):
                    head_chunks(it, "K1", k_hi, k_lo, "k", 1, 4 * c + 4)
                    masked_scores(it, 0)
                if it.has("A"):
                    for r in range(RT):
                        remainder(it, f"WH{r}", wh_hi_done, 2 * a + r + 1, wh_hi[:, r, :], wh_lo[:, r, :])
                    bank, _ = it.pj("S")
                    need(dve, s_hi_done, 2 * (a + 1))
                    s = pj[:, bank, 0:2 * RT].rearrange("p (r s) -> p r s", s=2)
                    dve.tensor_tensor(si_lo[:], s[:, :, 0], si_hi[:], ALU.subtract).then_inc(pj_free, 1)
                if it.has("C"):
                    split_probs(it, 0)
                    masked_scores(it, 1)
                if it.has("A"):
                    bank, _ = it.pj("ZT")
                    need(dve, z_relu_done, a + 1)
                    dve.scalar_tensor_tensor(out=z_e[:].rearrange("p r n -> p (r n)"), in0=pj[:, bank, :], scalar=LEAK / WS,
                                             in1=z_relu[:].rearrange("p r n -> p (r n)"), op0=ALU.mult, op1=ALU.add).then_inc(pj_free, 1)
                    need(dve, pj_free, it.pj("ZT")[1] + 1)
                    dve.tensor_reduce(z_negmax[:], z_e[:], AX_X, ALU.max, negate=True).then_inc(z_max_done, 1)
                if it.has("A"):
                    need(dve, z_exp_done, a + 1)
                    dve.reciprocal(z_inv[:], z_sum[:]).then_inc(z_inv_done, 1)
                    need(dve, z_inv_done, a + 1)
                    dve.tensor_scalar(z_inv16[:], z_inv[:], WS, None, ALU.mult).then_inc(z_scale_done, 1)
                if it.has("C"):
                    remainder(it, "V0", v_hi_done, 2 * c + 1, v_hi[:, 0, :], v_lo[:, 0, :])
                if it.has("A"):
                    need(dve, z_scale_done, a + 1)
                    for jt in range(RT):
                        need(dve, p0_hi_done, 2 * a + jt + 1)
                        dve.scalar_tensor_tensor(out=p0_lo[:, jt, :], in0=p0[:, jt, :], scalar=z_inv16[:, jt:jt + 1],
                                                 in1=p0_hi[:, jt, :], op0=ALU.mult, op1=ALU.subtract).then_inc(p0_lo_done, 1)
                if it.filling:
                    weight_remainders("q", "k")
                    scale_biases()
                if it.has("C"):
                    remainder(it, "V1", v_hi_done, 2 * c + 2, v_hi[:, 1, :], v_lo[:, 1, :])
                    split_probs(it, 1)
                if it.has("A"):
                    for r in range(RT):
                        bank, _ = it.pj(f"AT{r}")
                        need(dve, at_relu_done, 2 * a + r + 1)
                        dve.scalar_tensor_tensor(out=leak_part[:, r, :], in0=pj[:, bank, :], scalar=LEAK / WS ** 2,
                                                 in1=x_in[:, r, :], op0=ALU.mult, op1=ALU.add).then_inc(pj_free, 1)
                if it.has("C"):
                    masked_scores(it, 2)
                if it.has("A"):
                    stats_of(1, x1, x1_done, (2 * a + 1, 2 * a + 2))
                    carry_wait(1, stats_done[1], 2 * (a + 1))
                    ln_terms_of(1, a)
                if it.filling:
                    weight_remainders("v", "o")

                def result(r):
                    bank, use = it.pj(f"WO{r}")
                    need(dve, pj_ready, use + 1)
                    dve.scalar_tensor_tensor(out=y_lin[:, r, :], in0=pj[:, bank, :], scalar=1 / WS ** 2, in1=out_bias[:],
                                             op0=ALU.mult, op1=ALU.add).then_inc(pj_free, 1)
                    need(dve, pj_free, use + 1)
                    need(dve, y_stored, 16 * w)
                    need(dve, x1_kept_done, 2 * (w + 1))
                    dve.scalar_tensor_tensor(out=y_out[:, r, :], in0=y_lin[:, r, :], scalar=0.0,
                                             in1=x1_kept[1 - it.parity][:, r, :], op0=ALU.max, op1=ALU.add).then_inc(y_done, 1)

                if it.has("W"):
                    result(0)
                if it.has("C"):
                    split_probs(it, 2)
                    masked_scores(it, 3)
                if it.has("A"):
                    split_tr(it, "T1", halves(ht_hi[1]), halves(ht_lo[1]))
                if it.has("W"):
                    result(1)
                if it.has("C"):
                    split_probs(it, 3)
                    need(dve, exp_done, 4 * (c + 1))
                    dve.reciprocal(p_inv[:], p_sum[:]).then_inc(p_inv_done, 1)
                if it.has("N"):
                    stats_of(0, x_in, x_loaded, (16 * (f + 1), 16 * (f + 1)))
                    need(dve, stats_done[0], 2 * (f + 1))
                    need(dve, adj_loaded, 16 * (f + 1))
                    dve.tensor_scalar(mask[it.parity][:], adj_in[:], 0.0, MASKED, ALU.is_le, ALU.mult).then_inc(mask_done, 1)
                    ln_terms_of(0, f)
                if it.has("A"):
                    head_chunks(it, "Q0", q_hi, q_lo, "q", 0, 4 * a + 1)
                if it.has("C"):
                    need(dve, p_inv_done, c + 1)
                    need(dve, o_ready, c + 1)
                    for r in range(RT):
                        dve.tensor_tensor(o_n[:, r, :].rearrange("p (h d) -> p h d", h=NH),
                                          o_ps[:, r, :].rearrange("p (h d) -> p h d", h=NH),
                                          p_inv[:, r, :].unsqueeze(2).to_broadcast([P, NH, DH]), ALU.mult).then_inc(o_n_done, 1)
                if it.has("A"):
                    head_chunks(it, "Q1", q_hi, q_lo, "q", 1, 4 * a + 2)
                if it.has("C"):
                    split_tr(it, "OT", halves(ot_hi), halves(ot_lo))
                if it.has("A"):
                    head_chunks(it, "K0", k_hi, k_lo, "k", 0, 4 * a + 3)

            def head_chunks(it, step, hi, lo, m, half, value):
                bank, _ = it.pj(step)
                need(dve, qk_hi_done, value)
                for c2 in range(2):
                    c = 2 * half + c2
                    last = dve.scalar_tensor_tensor(out=lo[:, c, :], in0=pj[:, bank, c2 * N:(c2 + 1) * N],
                                                    scalar=bias[m][:, c:c + 1], in1=hi[:, c, :], op0=ALU.add, op1=ALU.subtract)
                last.then_inc(pj_free, 1)

            every_iteration(dve, body, {-1: set_up_first, 0: set_up_out_bias})


_INS = ["x", "adj", "L0_gnn_W", "L0_gnn_a", "L1_gnn_Wq", "L1_gnn_bq", "L1_gnn_Wk", "L1_gnn_bk", "L1_gnn_Wv", "L1_gnn_bv",
        "L1_gnn_Wo", "L1_gnn_bo"]


def kernel(**inputs):
    import numpy as _np
    import concourse.bacc as _bacc
    from concourse import mybir as _mybir
    from concourse.bass_utils import run_bass_kernel_spmd as _run

    nc = _bacc.Bacc("TRN2", target_bir_lowering=False, num_devices=1)
    arrays, args = {}, []
    for name in _INS:
        a = _np.ascontiguousarray(inputs[name])
        arrays[f"in_{name}_dram"] = a
        args.append(nc.dram_tensor(f"in_{name}_dram", a.shape, _mybir.dt.from_np(a.dtype), kind="ExternalInput").ap())
    shape = arrays["in_x_dram"].shape
    args.append(nc.dram_tensor("out_0_dram", shape, _mybir.dt.float32, kind="ExternalOutput").ap())
    build(nc, *args)
    r = _run(nc, [arrays], core_ids=[0])
    return r.results[0]["out_0_dram"]
```

```python
from contextlib import ExitStack

import concourse.bass as bass
from concourse import mybir

F32 = mybir.dt.float32
F16 = mybir.dt.float16
BF16 = mybir.dt.bfloat16
I32 = mybir.dt.int32
ACT = mybir.ActivationFunctionType
ALU = mybir.AluOpType
AX_X = mybir.AxisListType.X

P = 128
NH = 8
EPS = 1e-5
LEAK = 0.2
MASKED = -1e30
NO_SCORE = -3e38
WS = 16.0

TR_STEPS = ["T0", "PT0", "PT1", "PT2", "T1", "PT3", "OT"]
PJ_STEPS = ["K1", "WH0", "WH1", "S", "ZT", "V0", "V1", "AT0", "AT1", "WO0", "WO1", "Q0", "Q1", "K0"]
STEP_OF = {"T0": "A", "T1": "A", "OT": "C", "WH0": "A", "WH1": "A", "S": "A", "ZT": "A", "V0": "C", "V1": "C",
           "AT0": "A", "AT1": "A", "WO0": "W", "WO1": "W", "Q0": "A", "Q1": "A", "K0": "A", "K1": "C",
           "PT0": "C", "PT1": "C", "PT2": "C", "PT3": "C"}


class Iteration:

    def __init__(self, n, parity, stages, graphs):
        self.n, self.parity, self.stages = n, parity, stages
        self.filling = "A" in stages and "C" not in stages
        self.first_attention = stages == "ACN"
        self.tr_before, self.pj_before = self.uses_before(n, graphs)
        self.pj_parity = self.pj_before % 2 if isinstance(n, int) else 1

    @staticmethod
    def uses_before(n, graphs):
        if isinstance(n, int) and n < 1:
            return {-2: (0, 0), -1: (0, 0), 0: (2, 9)}[n]
        if isinstance(n, int) and n == graphs:
            return 2 + 7 * (n - 1) + 5, 14 * (n - 1) + 7 + 5
        return 2 + 7 * n, 14 * n + 7

    def has(self, stage):
        return stage in self.stages

    def tr(self, step):
        return self.tr_before + [s for s in TR_STEPS if self.has(STEP_OF[s])].index(step)

    def pj(self, step):
        at = [s for s in PJ_STEPS if self.has(STEP_OF[s])].index(step)
        return (self.pj_parity + at) % 2, self.pj_before + at


def need(eng, sem, value):
    if isinstance(value, int) and value <= 0:
        return
    eng.wait_ge(sem, value)


def build(nc, x, adj, w_gat, a_gat, wq, bq, wk, bk, wv, bv, wo, bo, out):
    B, N, D = x.shape
    KC = D // P
    RT = N // P
    DH = D // NH
    SCORE = float(DH) ** -0.5 / (WS * WS)
    assert (N, D, DH) == (256, 512, 64) and B >= 6 and B % 2 == 0

    with ExitStack() as ctx:
        def sb(name, shape, dt):
            return ctx.enter_context(nc.sbuf_tensor(name, shape, dt))

        def sem(name):
            return ctx.enter_context(nc.semaphore(name))

        tr = ctx.enter_context(nc.psum_tensor("tr", [P, 2, 512], F32))
        lg = ctx.enter_context(nc.psum_tensor("lg", [P, 2, 512], F32))
        pj = ctx.enter_context(nc.psum_tensor("pj", [P, 2, 512], F32))
        o_ps = ctx.enter_context(nc.psum_tensor("o_ps", [P, RT, 512], F32))

        id32 = sb("id32", [P, P], F32)
        id16 = sb("id16", [P, P], F16)
        idbf = sb("idbf", [P, P], BF16)
        neg_half = sb("neg_half", [P, RT], F32)
        names = ("gat", "q", "k", "v", "o")
        w_dram = dict(zip(names, (w_gat, wq, wk, wv, wo)))
        w_raw = {m: sb(f"w_raw_{m}", [P, KC, D], F32) for m in names}
        w_hi = {m: sb(f"w_hi_{m}", [P, KC, D], F16) for m in names}
        w_lo = {m: sb(f"w_lo_{m}", [P, KC, D], F16) for m in names}
        a_rows = sb("a_rows", [P, 2, D], F32)
        wa = sb("wa", [P, KC, 2], F32)
        wa_parts = sb("wa_parts", [P, KC, 2, 2], F16)
        wa_hi, wa_lo = wa_parts[:, :, 0, :], wa_parts[:, :, 1, :]
        wa_prod = sb("wa_prod", [P, 2, D], F32)
        bias_raw = {m: sb(f"bias_raw_{m}", [P, KC], F32) for m in "qkv"}
        bias = {m: sb(f"bias_{m}", [P, KC], F32) for m in "qkv"}
        bv_hi = sb("bv_hi", [P, KC], F16)
        bv_lo = sb("bv_lo", [P, KC], F16)
        bo_rows = sb("bo_rows", [P, D], F32)
        out_bias = sb("out_bias", [P, D], F32)

        x_in = sb("x_in", [P, RT, D], F32)
        adj_in = sb("adj_in", [P, RT, N], I32)
        mask = [sb(f"mask{i}", [P, RT, N], BF16) for i in range(2)]
        stats = [sb(f"stats{i}", [P, RT, 6], F32) for i in range(2)]
        moments = [sb(f"moments{i}", [P, RT, 2], F32) for i in range(2)]
        neg_mean = [sb(f"neg_mean{i}", [P, RT], F32) for i in range(2)]
        var_eps = [sb(f"var_eps{i}", [P, RT], F32) for i in range(2)]
        shift = [sb(f"shift{i}", [P, RT], F32) for i in range(2)]
        rstd = [sb(f"rstd{i}", [P, RT], F32) for i in range(2)]
        hn = [sb(f"hn{i}", [P, RT, D], F32) for i in range(2)]
        ht_hi = [sb(f"ht_hi{i}", [P, KC, N], F16) for i in range(2)]
        ht_lo = [sb(f"ht_lo{i}", [P, KC, N], F16) for i in range(2)]

        wh_hi = sb("wh_hi", [P, RT, D], F16)
        wh_lo = sb("wh_lo", [P, RT, D], F16)
        s_terms = sb("s_terms", [P, RT, 2], F32)
        si_hi = sb("si_hi", [P, RT], F16)
        si_lo = sb("si_lo", [P, RT], F16)
        sj_bias = sb("sj_bias", [P, RT], F32)
        z_relu = sb("z_relu", [P, RT, N], F32)
        z_e = sb("z_e", [P, RT, N], F32)
        z_negmax = sb("z_negmax", [P, RT], F32)
        z_sum = sb("z_sum", [P, RT], F32)
        z_inv = sb("z_inv", [P, RT], F32)
        z_inv16 = sb("z_inv16", [P, RT], F32)
        p0 = sb("p0", [P, RT, N], F32)
        p0_hi = sb("p0_hi", [P, RT, N], F16)
        p0_lo = sb("p0_lo", [P, RT, N], F16)
        relu_part = sb("relu_part", [P, RT, D], F32)
        leak_part = sb("leak_part", [P, RT, D], F32)
        x1 = sb("x1", [P, RT, D], F32)
        x1_kept = [sb(f"x1_kept{i}", [P, RT, D], F32) for i in range(2)]

        q_hi = sb("q_hi", [P, KC, N], F16)
        q_lo = sb("q_lo", [P, KC, N], F16)
        k_hi = sb("k_hi", [P, KC, N], F16)
        k_lo = sb("k_lo", [P, KC, N], F16)
        v_hi = sb("v_hi", [P, RT, D], F16)
        v_lo = sb("v_lo", [P, RT, D], F16)
        negmax = sb("negmax", [P, 4], F32)
        scores_neg = sb("scores_neg", [P, 4, N], F32)
        wait_carrier = sb("wait_carrier", [P, 2], F32)
        p_exp = sb("p_exp", [P, 4, N], F32)
        p_sum = sb("p_sum", [P, RT, NH], F32)
        p_inv = sb("p_inv", [P, RT, NH], F32)
        pt_hi = [sb(f"pt_hi{i}", [P, 2, 512], F16) for i in range(2)]
        pt_lo = [sb(f"pt_lo{i}", [P, 2, 512], F16) for i in range(2)]
        o_n = sb("o_n", [P, RT, D], F32)
        ot_hi = sb("ot_hi", [P, KC, N], F16)
        ot_lo = sb("ot_lo", [P, KC, N], F16)
        y_lin = sb("y_lin", [P, RT, D], F32)
        y_out = sb("y_out", [P, RT, D], F32)

        ident_zeroed = sem("ident_zeroed")
        ident_ready = sem("ident_ready")
        w_loaded = {m: sem(f"w_loaded_{m}") for m in names}
        a_loaded = sem("a_loaded")
        bias_loaded = sem("bias_loaded")
        w_hi_done = sem("w_hi_done")
        w_lo_done = sem("w_lo_done")
        wa_summed = sem("wa_summed")
        wa_hi_done = sem("wa_hi_done")
        wa_lo_done = sem("wa_lo_done")
        bias_scaled = sem("bias_scaled")
        bv_hi_done = sem("bv_hi_done")
        bv_lo_done = sem("bv_lo_done")
        out_bias_summed = sem("out_bias_summed")
        out_bias_done = sem("out_bias_done")
        x_loaded = sem("x_loaded")
        adj_loaded = sem("adj_loaded")
        mask_done = sem("mask_done")
        stats_done = [sem(f"stats_done{i}") for i in range(2)]
        moments_done = [sem(f"moments_done{i}") for i in range(2)]
        ln_terms = [sem(f"ln_terms{i}") for i in range(2)]
        rstd_done = [sem(f"rstd_done{i}") for i in range(2)]
        shift_done = [sem(f"shift_done{i}") for i in range(2)]
        hn_done = [sem(f"hn_done{i}") for i in range(2)]
        tr_ready, tr_hi, tr_free = sem("tr_ready"), sem("tr_hi"), sem("tr_free")
        pj_ready, pj_free = sem("pj_ready"), sem("pj_free")
        wh_hi_done = sem("wh_hi_done")
        s_hi_done = sem("s_hi_done")
        s_lo_done = sem("s_lo_done")
        z_relu_done = sem("z_relu_done")
        z_max_done = sem("z_max_done")
        z_exp_done = sem("z_exp_done")
        z_inv_done = sem("z_inv_done")
        z_scale_done = sem("z_scale_done")
        p0_hi_done = sem("p0_hi_done")
        p0_lo_done = sem("p0_lo_done")
        at_relu_done = sem("at_relu_done")
        x1_done = sem("x1_done")
        x1_kept_done = sem("x1_kept_done")
        qk_hi_done = sem("qk_hi_done")
        v_hi_done = sem("v_hi_done")
        lg_ready = sem("lg_ready")
        masked_done = sem("masked_done")
        exp_done = sem("exp_done")
        o_ready = sem("o_ready")
        p_inv_done = sem("p_inv_done")
        o_n_done = sem("o_n_done")
        y_done = sem("y_done")
        y_stored = sem("y_stored")

        x_rows = x.rearrange("b (r p) d -> b p r d", p=P)
        adj_rows = adj.rearrange("b (r p) n -> b p r n", p=P)
        out_rows = out.rearrange("b (r p) d -> b p r d", p=P)

        def every_iteration(eng, body, before=None):
            for n, stages in ((-2, "N"), (-1, "AN"), (0, "ACN"), (1, "ACWN")):
                if before and n in before:
                    before[n]()
                body(Iteration(n, n % 2, stages, B))
            with eng.Fori(1, B // 2 - 1) as pair:
                for step in range(2):
                    body(Iteration(2 * pair + step, step, "ACWN", B))
            for n, stages in ((B - 2, "ACW"), (B - 1, "CW"), (B, "W")):
                body(Iteration(n, n % 2, stages, B))

        block = ctx.enter_context(nc.Block())

        @block.sync
        def _(sp):
            sp.dma_start(x_in[:], x_rows[0]).then_inc(x_loaded, 16)
            sp.dma_start(adj_in[:], adj_rows[0]).then_inc(adj_loaded, 16)
            sp.dma_start(w_raw["gat"][:], w_dram["gat"].rearrange("(c p) n -> p c n", p=P)).then_inc(w_loaded["gat"], 16)
            a_bcast = a_gat.rearrange("(s d) one -> one s d", s=2).to_broadcast([P, 2, D])
            sp.dma_start(a_rows[:], a_bcast).then_inc(a_loaded, 16)
            for m in ("q", "k", "v", "o"):
                sp.dma_start(w_raw[m][:], w_dram[m].rearrange("(c p) n -> p c n", p=P)).then_inc(w_loaded[m], 16)
            with nc.allow_non_contiguous_dma(reason="three bias vectors, once"):
                for m, b in (("q", bq), ("k", bk), ("v", bv)):
                    sp.dma_start(bias_raw[m][:], b.rearrange("(c p) -> p c", p=P)).then_inc(bias_loaded, 16)
            sp.dma_start(bo_rows[:], bo.rearrange("(one d) -> one d", one=1).to_broadcast([P, D])).then_inc(bias_loaded, 16)

            def body(it):
                n = it.n
                f, w = n + 2, n - 1
                if it.has("N") and it.has("A"):
                    need(sp, mask_done, f)
                    sp.dma_start(adj_in[:], adj_rows[bass.ds(f, 1)].rearrange("b p r n -> p (b r) n")).then_inc(adj_loaded, 16)
                    need(sp, pj_free, it.pj("AT1")[1] + 1)
                    sp.dma_start(x_in[:], x_rows[bass.ds(f, 1)].rearrange("b p r d -> p (b r) d")).then_inc(x_loaded, 16)
                if it.has("W"):
                    need(sp, y_done, 2 * (w + 1))
                    sp.dma_start(out_rows[bass.ds(w, 1)].rearrange("b p r d -> p (b r) d"), y_out[:]).then_inc(y_stored, 16)

            every_iteration(sp, body)
            sp.wait_ge(y_stored, 16 * B)

        @block.gpsimd
        def _(pool):
            pool.memset(id32[:], 0.0).then_inc(ident_zeroed, 1)
            pool.memset(neg_half[:], -0.5).then_inc(ident_zeroed, 1)
            pool.wait_ge(ident_zeroed, 2)
            pool.affine_select(out=id32[:], in_=id32[:], compare_op=ALU.not_equal, fill=1.0, base=0,
                               pattern=[[-1, P]], channel_multiplier=1).then_inc(ident_zeroed, 1)
            pool.wait_ge(ident_zeroed, 3)
            pool.tensor_copy(id16[:], id32[:]).then_inc(ident_ready, 1)
            pool.tensor_copy(idbf[:], id32[:]).then_inc(ident_ready, 1)

            def norm_factors(ln, g):
                need(pool, ln_terms[ln], 2 * (g + 1))
                pool.tensor_tensor(rstd[ln][:], var_eps[ln][:], neg_half[:], ALU.pow).then_inc(rstd_done[ln], 1)
                need(pool, rstd_done[ln], g + 1)
                pool.tensor_tensor(shift[ln][:], neg_mean[ln][:], rstd[ln][:], ALU.mult).then_inc(shift_done[ln], 1)

            def body(it):
                n = it.n
                a, f, w = n + 1, n + 2, n - 1
                if it.has("A"):
                    for r in range(RT):
                        need(pool, pj_free, it.pj(f"AT{r}")[1] + 1)
                        need(pool, hn_done[1], 2 * a)
                        pool.tensor_tensor(x1[:, r, :], relu_part[:, r, :], leak_part[:, r, :], ALU.add).then_inc(x1_done, 1)
                    norm_factors(1, a)
                    if it.has("W"):
                        need(pool, y_done, 2 * (w + 1))
                    for r in range(RT):
                        pool.tensor_tensor(x1_kept[1 - it.parity][:, r, :], relu_part[:, r, :], leak_part[:, r, :],
                                           ALU.add).then_inc(x1_kept_done, 1)
                if it.has("N"):
                    norm_factors(0, f)

            every_iteration(pool, body)

        @block.tensor
        def _(pe):
            def to_transposed(step, it, source, ready, value):
                need(pe, ready, value)
                for bank in range(2):
                    need(pe, tr_free, 2 * (it.tr(step) - 1) + bank + 1)
                    for c in range(2):
                        for r in range(RT):
                            last = pe.transpose(tr[:, bank, c * N + r * P:c * N + (r + 1) * P],
                                                source[:, r, (2 * bank + c) * P:(2 * bank + c + 1) * P], id32[:])
                    last.then_inc(tr_ready, 1)

            def split_product(dst, pairs, first=True, final=True):
                for i, (s_hi, s_lo, m_hi, m_lo) in enumerate(pairs):
                    pe.matmul(dst, s_hi, m_hi, start=(first and i == 0), stop=False)
                    pe.matmul(dst, s_hi, m_lo, start=False, stop=False)
                    last = pe.matmul(dst, s_lo, m_hi, start=False, stop=(final and i == len(pairs) - 1))
                return last

            def take_pj(it, step):
                bank, use = it.pj(step)
                need(pe, pj_free, use - 1)
                return pj[:, bank, :]

            def rows_times_weight(it, step, r, t_hi, t_lo, m, chunks=range(KC)):
                first, final = chunks[0] == 0, chunks[-1] == KC - 1
                dst = take_pj(it, step) if first else pj[:, it.pj(step)[0], :]
                rows = slice(r * P, (r + 1) * P)
                last = split_product(dst, [(t_hi[:, c, rows], t_lo[:, c, rows], w_hi[m][:, c, :], w_lo[m][:, c, :])
                                           for c in chunks], first, final)
                if final:
                    last.then_inc(pj_ready, 1)

            def scores(it, u):
                n = it.n
                if u == 0:
                    need(pe, pj_free, it.pj_before)
                if u == 2:
                    need(pe, pj_free, it.pj("K1")[1] + 1)
                need(pe, masked_done, 8 * n + 2 * u)
                for r in range(RT):
                    for i, (qq, kk) in enumerate(((q_hi, k_hi), (q_hi, k_lo), (q_lo, k_hi))):
                        for j in range(2):
                            h = slice(DH * j, DH * (j + 1))
                            last = pe.matmul(lg[:, j, r * N:(r + 1) * N], qq[h, u, r * P:(r + 1) * P], kk[h, u, :],
                                             start=(i == 0), stop=(i == 2))
                last.then_inc(lg_ready, 1)

            def transpose_probs(it, u):
                use = it.tr(f"PT{u}")
                for j in range(2):
                    need(pe, exp_done, 8 * it.n + 2 * u + j + 1)
                    need(pe, tr_free, 2 * (use - 1) + j + 1)
                    for kt in range(RT):
                        for r in range(RT):
                            last = pe.transpose(tr[:, j, kt * N + r * P:kt * N + (r + 1) * P],
                                                p_exp[:, 2 * j + r, kt * P:(kt + 1) * P], id32[:])
                    last.then_inc(tr_ready, 1)

            def probs_times_v(it, u):
                n = it.n
                if u == 0:
                    need(pe, o_n_done, 2 * n)
                    if it.first_attention:
                        pe.wait_ge(out_bias_done, 1)
                    need(pe, pj_free, it.pj("V1")[1] + 1)
                need(pe, tr_free, 2 * it.tr(f"PT{u}") + 2)
                for j in range(2):
                    h = slice((2 * u + j) * DH, (2 * u + j + 1) * DH)
                    for r in range(RT):
                        cols = [slice(kt * N + r * P, kt * N + (r + 1) * P) for kt in range(RT)]
                        last = split_product(o_ps[:, r, h], [(pt_hi[u % 2][:, j, cols[kt]], pt_lo[u % 2][:, j, cols[kt]],
                                                              v_hi[:, kt, h], v_lo[:, kt, h]) for kt in range(RT)])
                if u == NH // 2 - 1:
                    last.then_inc(o_ready, 1)

            def head_columns(it, step, m, half):
                dst = take_pj(it, step)
                for c2 in range(2):
                    cols = slice((2 * half + c2) * P, (2 * half + c2 + 1) * P)
                    last = split_product(dst[:, c2 * N:(c2 + 1) * N],
                                         [(w_hi[m][:, c, cols], w_lo[m][:, c, cols], ht_hi[1][:, c, :], ht_lo[1][:, c, :])
                                          for c in range(KC)])
                last.then_inc(pj_ready, 1)

            def identities():
                pe.wait_ge(ident_ready, 2)

            def set_up_out_bias():
                pe.wait_ge(w_lo_done, 5)
                pe.wait_ge(bv_lo_done, 1)
                bv_pairs = [(b[:, c:c + 1].to_broadcast([P, P])) for c in range(KC) for b in (bv_hi, bv_lo)]
                split_product(o_ps[:, 0, :], [(bv_pairs[2 * c], bv_pairs[2 * c + 1], w_hi["o"][:, c, :], w_lo["o"][:, c, :])
                                              for c in range(KC)]).then_inc(out_bias_summed, 1)

            def body(it):
                n = it.n
                a, c = n + 1, n
                if it.has("A"):
                    to_transposed("T0", it, hn[0], hn_done[0], 2 * (a + 1))
                if it.has("C"):
                    head_columns(it, "K1", "k", 1)
                    scores(it, 0)
                if it.first_attention:
                    set_up_out_bias()
                if it.has("A"):
                    need(pe, tr_free, 2 * it.tr("T0") + 2)
                    if it.filling:
                        pe.wait_ge(w_lo_done, 1)
                    rows_times_weight(it, "WH0", 0, ht_hi[0], ht_lo[0], "gat")
                    rows_times_weight(it, "WH1", 1, ht_hi[0], ht_lo[0], "gat")
                    if it.filling:
                        pe.wait_ge(wa_lo_done, 1)
                    dst = take_pj(it, "S")
                    for r in range(RT):
                        rows = slice(r * P, (r + 1) * P)
                        both, heads = dst[:, 4 * r:4 * r + 4], dst[:, 4 * r:4 * r + 2]
                        pe.matmul(both, ht_hi[0][:, 0, rows], wa_parts[:, 0, :, :], start=True, stop=False)
                        for k in range(KC):
                            pe.matmul(heads, ht_lo[0][:, k, rows], wa_hi[:, k, :], start=False, stop=False)
                        for k in range(1, KC):
                            last = pe.matmul(both, ht_hi[0][:, k, rows], wa_parts[:, k, :, :], start=False, stop=(k == KC - 1))
                    last.then_inc(pj_ready, 1)
                if it.has("C"):
                    transpose_probs(it, 0)
                    scores(it, 1)
                if it.has("A"):
                    dst = take_pj(it, "ZT")
                    need(pe, mask_done, a + 1)
                    need(pe, s_lo_done, a + 1)
                    for jt in range(RT):
                        for r in range(RT):
                            part = dst[:, jt * N + r * P:jt * N + (r + 1) * P]
                            pe.matmul(part, mask[1 - it.parity][:, r, jt * P:(jt + 1) * P], idbf[:], start=True, stop=False)
                            pe.matmul(part, si_hi[:, r:r + 1].to_broadcast([P, P]), id16[:], start=False, stop=False)
                            last = pe.matmul(part, si_lo[:, r:r + 1].to_broadcast([P, P]), id16[:], start=False, stop=True)
                    last.then_inc(pj_ready, 1)
                if it.has("C"):
                    rows_times_weight(it, "V0", 0, ht_hi[1], ht_lo[1], "v")
                    rows_times_weight(it, "V1", 1, ht_hi[1], ht_lo[1], "v")
                    transpose_probs(it, 1)
                if it.has("A"):
                    need(pe, p0_hi_done, 2 * (a + 1))
                    for r in range(RT):
                        dst = take_pj(it, f"AT{r}")
                        rows = slice(r * P, (r + 1) * P)
                        for jt in range(RT):
                            pe.matmul(dst, p0_hi[:, jt, rows], wh_hi[:, jt, :], start=(jt == 0), stop=False)
                            pe.matmul(dst, p0_hi[:, jt, rows], wh_lo[:, jt, :], start=False, stop=False)
                        for jt in range(RT):
                            if r == 0:
                                need(pe, p0_lo_done, 2 * a + jt + 1)
                            last = pe.matmul(dst, p0_lo[:, jt, rows], wh_hi[:, jt, :], start=False, stop=(jt == RT - 1))
                        last.then_inc(pj_ready, 1)
                if it.has("C"):
                    scores(it, 2)
                    probs_times_v(it, 0)
                    probs_times_v(it, 1)
                if it.has("W"):
                    need(pe, tr_free, 2 * it.tr_before)
                    rows_times_weight(it, "WO0", 0, ot_hi, ot_lo, "o")
                if it.has("C"):
                    transpose_probs(it, 2)
                    scores(it, 3)
                if it.has("W"):
                    rows_times_weight(it, "WO1", 1, ot_hi, ot_lo, "o", range(0, 1))
                if it.has("A"):
                    to_transposed("T1", it, hn[1], hn_done[1], 2 * (a + 1))
                if it.has("W"):
                    rows_times_weight(it, "WO1", 1, ot_hi, ot_lo, "o", range(1, KC))
                if it.has("C"):
                    probs_times_v(it, 2)
                    transpose_probs(it, 3)
                if it.has("A"):
                    if it.filling:
                        pe.wait_ge(w_lo_done, 2)
                    need(pe, tr_free, 2 * it.tr("T1") + 2)
                    head_columns(it, "Q0", "q", 0)
                if it.has("C"):
                    probs_times_v(it, 3)
                if it.has("A"):
                    head_columns(it, "Q1", "q", 1)
                if it.has("C"):
                    to_transposed("OT", it, o_n, o_n_done, 2 * (c + 1))
                if it.has("A"):
                    if it.filling:
                        pe.wait_ge(w_lo_done, 3)
                    head_columns(it, "K0", "k", 0)

            every_iteration(pe, body, {-1: identities})

        @block.scalar
        def _(act):
            def split_tr(it, step, hi, func):
                for bank in range(2):
                    need(act, tr_ready, 2 * it.tr(step) + bank + 1)
                    act.activation(hi(bank), tr[:, bank, :], func).then_inc(tr_hi, 1)

            def split_probs(it, u):
                split_tr(it, f"PT{u}", lambda j: pt_hi[u % 2][:, j, :], ACT.Copy)

            def normalise(g):
                need(act, shift_done[0], g + 1)
                for r in range(RT):
                    act.activation(hn[0][:, r, :], x_in[:, r, :], ACT.Identity, bias=shift[0][:, r:r + 1],
                                   scale=rstd[0][:, r:r + 1]).then_inc(hn_done[0], 1)

            def exps(it, u, heads=(0, 1)):
                for j in heads:
                    need(act, masked_done, 8 * it.n + 2 * u + j + 1)
                    for r in range(RT):
                        last = act.activation(p_exp[:, 2 * j + r, :], scores_neg[:, 2 * j + r, :], ACT.Exp,
                                              bias=negmax[:, 2 * j + r:2 * j + r + 1], scale=-1.0,
                                              accum_out=p_sum[:, r, 2 * u + j:2 * u + j + 1])
                    last.then_inc(exp_done, 1)

            def bank_of(it, step):
                bank, use = it.pj(step)
                need(act, pj_ready, use + 1)
                return pj[:, bank, :]

            def head_chunks(it, step, hi, m, half):
                bank = bank_of(it, step)
                for c2 in range(2):
                    c = 2 * half + c2
                    last = act.activation(hi[:, c, :], bank[:, c2 * N:(c2 + 1) * N], ACT.Identity, bias=bias[m][:, c:c + 1])
                last.then_inc(qk_hi_done, 1)

            def weight_heads(*which):
                for m in which:
                    act.wait_ge(w_loaded[m], 16)
                    act.activation(w_hi[m][:], w_raw[m][:], ACT.Copy, scale=WS).then_inc(w_hi_done, 1)

            def wa_head():
                act.wait_ge(wa_summed, 2 * KC)
                act.activation(wa_hi, wa[:], ACT.Copy).then_inc(wa_hi_done, 1)

            def bv_head():
                act.wait_ge(bias_scaled, 3)
                act.activation(bv_hi[:], bias["v"][:], ACT.Copy).then_inc(bv_hi_done, 1)

            def body(it):
                n = it.n
                a = n + 1
                if it.has("A"):
                    split_tr(it, "T0", lambda bank: ht_hi[0][:, 2 * bank:2 * bank + 2, :], ACT.Relu)
                if it.filling:
                    wa_head()
                if it.has("C"):
                    head_chunks(it, "K1", k_hi, "k", 1)
                    exps(it, 0, (0,))
                if it.has("A"):
                    act.activation(wh_hi[:, 0, :], bank_of(it, "WH0"), ACT.Copy).then_inc(wh_hi_done, 1)
                if it.has("C"):
                    exps(it, 0, (1,))
                if it.has("A"):
                    act.activation(wh_hi[:, 1, :], bank_of(it, "WH1"), ACT.Copy).then_inc(wh_hi_done, 1)
                    need(act, pj_free, it.pj("S")[1] + 1)
                    act.activation(si_hi[:], s_terms[:, :, 0], ACT.Copy).then_inc(s_hi_done, 1)
                    act.activation(sj_bias[:], s_terms[:, :, 1], ACT.Copy, scale=(1 - LEAK) / WS).then_inc(s_hi_done, 1)
                if it.has("C"):
                    split_probs(it, 0)
                if it.has("A"):
                    z = bank_of(it, "ZT")
                    need(act, s_hi_done, 2 * (a + 1))
                    for jt in range(RT):
                        last = act.activation(z_relu[:, jt, :], z[:, jt * N:(jt + 1) * N], ACT.Relu,
                                              bias=sj_bias[:, jt:jt + 1], scale=(1 - LEAK) / WS)
                    last.then_inc(z_relu_done, 1)
                if it.has("C"):
                    exps(it, 1)
                if it.has("A"):
                    need(act, z_max_done, a + 1)
                    for jt in range(RT):
                        last = act.activation(p0[:, jt, :], z_e[:, jt, :], ACT.Exp, bias=z_negmax[:, jt:jt + 1],
                                              accum_out=z_sum[:, jt:jt + 1])
                    last.then_inc(z_exp_done, 1)
                if it.has("C"):
                    act.activation(v_hi[:, 0, :], bank_of(it, "V0"), ACT.Copy).then_inc(v_hi_done, 1)
                if it.filling:
                    weight_heads("q")
                if it.has("C"):
                    act.activation(v_hi[:, 1, :], bank_of(it, "V1"), ACT.Copy).then_inc(v_hi_done, 1)
                    split_probs(it, 1)
                if it.has("A"):
                    for r in range(RT):
                        bank = bank_of(it, f"AT{r}")
                        need(act, x1_kept_done, 2 * a)
                        act.activation(relu_part[:, r, :], bank, ACT.Relu, scale=(1 - LEAK) / WS ** 2).then_inc(at_relu_done, 1)
                if it.filling:
                    weight_heads("k", "v")
                if it.has("C"):
                    exps(it, 2)
                    split_probs(it, 2)
                if it.has("A"):
                    split_tr(it, "T1", lambda bank: ht_hi[1][:, 2 * bank:2 * bank + 2, :], ACT.Relu)
                if it.filling:
                    bv_head()
                    weight_heads("o")
                if it.has("C"):
                    exps(it, 3)
                    split_probs(it, 3)
                if it.has("A"):
                    head_chunks(it, "Q0", q_hi, "q", 0)
                if it.has("N"):
                    if it.has("A"):
                        need(act, tr_ready, 2 * it.tr("T0") + 2)
                    normalise(n + 2)
                if it.has("C"):
                    split_tr(it, "OT", lambda bank: ot_hi[:, 2 * bank:2 * bank + 2, :], ACT.Copy)
                if it.has("A"):
                    head_chunks(it, "Q1", q_hi, "q", 1)
                if it.has("A"):
                    head_chunks(it, "K0", k_hi, "k", 0)

            every_iteration(act, body, {-1: lambda: weight_heads("gat")})

        @block.vector
        def _(dve):
            def carry_wait(cell, sem, value):
                need(dve, sem, value)
                dve.memset(wait_carrier[:, cell:cell + 1], 0.0)

            def halves(t):
                return lambda bank: t[:, 2 * bank:2 * bank + 2, :].rearrange("p c n -> p (c n)")

            def split_tr(it, step, hi, lo, relu=False):
                for bank in range(2):
                    need(dve, tr_hi, 2 * it.tr(step) + bank + 1)
                    if relu:
                        dve.scalar_tensor_tensor(out=lo(bank), in0=tr[:, bank, :], scalar=0.0, in1=hi(bank), op0=ALU.max,
                                                 op1=ALU.subtract).then_inc(tr_free, 1)
                    else:
                        dve.tensor_tensor(lo(bank), tr[:, bank, :], hi(bank), ALU.subtract).then_inc(tr_free, 1)

            def split_probs(it, u):
                split_tr(it, f"PT{u}", lambda j: pt_hi[u % 2][:, j, :], lambda j: pt_lo[u % 2][:, j, :])

            def remainder(it, step, hi_done, value, hi, lo):
                bank, _ = it.pj(step)
                need(dve, hi_done, value)
                dve.tensor_tensor(lo, pj[:, bank, :], hi, ALU.subtract).then_inc(pj_free, 1)

            def masked_scores(it, u):
                need(dve, lg_ready, 4 * it.n + u + 1)
                carry_wait(0, exp_done, 8 * it.n + 2 * u)
                for j in range(2):
                    for r in range(RT):
                        last = dve.tensor_tensor_reduce(out=scores_neg[:, 2 * j + r, :], in0=lg[:, j, r * N:(r + 1) * N],
                                                        in1=mask[it.parity][:, r, :], scale=-SCORE, scalar=-NO_SCORE,
                                                        op0=ALU.add, op1=ALU.min, accum_out=negmax[:, 2 * j + r:2 * j + r + 1])
                    last.then_inc(masked_done, 1)

            def stats_of(ln, source, ready, values):
                for r in range(RT):
                    need(dve, ready, values[r])
                    dve.bn_stats(stats[ln][:, r, :], source[:, r, :]).then_inc(stats_done[ln], 1)

            def ln_terms_of(ln, g):
                for r in range(RT):
                    dve.bn_aggr(moments[ln][:, r, :], stats[ln][:, r, :]).then_inc(moments_done[ln], 1)
                need(dve, moments_done[ln], 2 * (g + 1))
                need(dve, shift_done[ln], g)
                dve.tensor_scalar(neg_mean[ln][:], moments[ln][:, :, 0], -1.0, None, ALU.mult).then_inc(ln_terms[ln], 1)
                dve.tensor_scalar(var_eps[ln][:], moments[ln][:, :, 1], EPS, None, ALU.add).then_inc(ln_terms[ln], 1)

            def head_chunks(it, step, hi, lo, m, half, value):
                bank, _ = it.pj(step)
                need(dve, qk_hi_done, value)
                for c2 in range(2):
                    c = 2 * half + c2
                    last = dve.scalar_tensor_tensor(out=lo[:, c, :], in0=pj[:, bank, c2 * N:(c2 + 1) * N],
                                                    scalar=bias[m][:, c:c + 1], in1=hi[:, c, :], op0=ALU.add, op1=ALU.subtract)
                last.then_inc(pj_free, 1)

            def result(it, r):
                w = it.n - 1
                bank, use = it.pj(f"WO{r}")
                need(dve, pj_ready, use + 1)
                dve.scalar_tensor_tensor(out=y_lin[:, r, :], in0=pj[:, bank, :], scalar=1 / WS ** 2, in1=out_bias[:],
                                         op0=ALU.mult, op1=ALU.add).then_inc(pj_free, 1)
                need(dve, pj_free, use + 1)
                need(dve, y_stored, 16 * w)
                need(dve, x1_kept_done, 2 * (w + 1))
                dve.scalar_tensor_tensor(out=y_out[:, r, :], in0=y_lin[:, r, :], scalar=0.0,
                                         in1=x1_kept[1 - it.parity][:, r, :], op0=ALU.max, op1=ALU.add).then_inc(y_done, 1)

            def weight_remainders(*which):
                for m in which:
                    dve.wait_ge(w_hi_done, names.index(m) + 1)
                    dve.scalar_tensor_tensor(out=w_lo[m][:].rearrange("p c n -> p (c n)"),
                                             in0=w_raw[m][:].rearrange("p c n -> p (c n)"), scalar=WS,
                                             in1=w_hi[m][:].rearrange("p c n -> p (c n)"), op0=ALU.mult,
                                             op1=ALU.subtract).then_inc(w_lo_done, 1)

            def attention_vectors():
                dve.wait_ge(w_loaded["gat"], 16)
                dve.wait_ge(a_loaded, 16)
                for c in range(KC):
                    for s in range(2):
                        if c:
                            dve.wait_ge(wa_summed, 2 * (c - 1) + s + 1)
                        dve.scalar_tensor_tensor(out=wa_prod[:, s, :], in0=w_raw["gat"][:, c, :], scalar=WS, in1=a_rows[:, s, :],
                                                 op0=ALU.mult, op1=ALU.mult, accum_out=wa[:, c, s:s + 1]).then_inc(wa_summed, 1)
                dve.wait_ge(wa_hi_done, 1)
                dve.tensor_tensor(wa_lo, wa[:], wa_hi, ALU.subtract).then_inc(wa_lo_done, 1)

            def scale_biases():
                dve.wait_ge(bias_loaded, 64)
                for m in "qkv":
                    dve.tensor_scalar(bias[m][:], bias_raw[m][:], WS, None, ALU.mult).then_inc(bias_scaled, 1)

            def bv_remainder():
                dve.wait_ge(bv_hi_done, 1)
                dve.tensor_tensor(bv_lo[:], bias["v"][:], bv_hi[:], ALU.subtract).then_inc(bv_lo_done, 1)

            def set_up_out_bias():
                dve.wait_ge(out_bias_summed, 1)
                dve.scalar_tensor_tensor(out=out_bias[:], in0=o_ps[:, 0, :], scalar=1 / WS ** 2, in1=bo_rows[:], op0=ALU.mult,
                                         op1=ALU.add).then_inc(out_bias_done, 1)

            def body(it):
                n = it.n
                a, c, f = n + 1, n, n + 2
                if it.has("A"):
                    split_tr(it, "T0", halves(ht_hi[0]), halves(ht_lo[0]), relu=True)
                if it.filling:
                    attention_vectors()
                if it.has("C"):
                    head_chunks(it, "K1", k_hi, k_lo, "k", 1, 4 * c + 4)
                    masked_scores(it, 0)
                if it.first_attention:
                    set_up_out_bias()
                if it.has("A"):
                    for r in range(RT):
                        remainder(it, f"WH{r}", wh_hi_done, 2 * a + r + 1, wh_hi[:, r, :], wh_lo[:, r, :])
                    bank, use = it.pj("S")
                    need(dve, pj_ready, use + 1)
                    dve.tensor_reduce(s_terms[:], pj[:, bank, 0:4 * RT].rearrange("p (r part s) -> p r s part", part=2, s=2),
                                      AX_X, ALU.add).then_inc(pj_free, 1)
                    need(dve, s_hi_done, 2 * (a + 1))
                    dve.tensor_tensor(si_lo[:], s_terms[:, :, 0], si_hi[:], ALU.subtract).then_inc(s_lo_done, 1)
                if it.has("C"):
                    split_probs(it, 0)
                    masked_scores(it, 1)
                if it.has("A"):
                    bank, _ = it.pj("ZT")
                    need(dve, z_relu_done, a + 1)
                    dve.scalar_tensor_tensor(out=z_e[:].rearrange("p r n -> p (r n)"), in0=pj[:, bank, :], scalar=LEAK / WS,
                                             in1=z_relu[:].rearrange("p r n -> p (r n)"), op0=ALU.mult, op1=ALU.add).then_inc(pj_free, 1)
                    need(dve, pj_free, it.pj("ZT")[1] + 1)
                    dve.tensor_reduce(z_negmax[:], z_e[:], AX_X, ALU.max, negate=True).then_inc(z_max_done, 1)
                    need(dve, z_exp_done, a + 1)
                    dve.reciprocal(z_inv[:], z_sum[:]).then_inc(z_inv_done, 1)
                    need(dve, z_inv_done, a + 1)
                    dve.tensor_scalar(z_inv16[:], z_inv[:], WS, None, ALU.mult).then_inc(z_scale_done, 1)
                    need(dve, z_scale_done, a + 1)
                    for jt in range(RT):
                        dve.tensor_scalar(p0_hi[:, jt, :], p0[:, jt, :], z_inv16[:, jt:jt + 1], None, ALU.mult).then_inc(p0_hi_done, 1)
                if it.has("C"):
                    remainder(it, "V0", v_hi_done, 2 * c + 1, v_hi[:, 0, :], v_lo[:, 0, :])
                if it.has("A"):
                    for jt in range(RT):
                        need(dve, p0_hi_done, 2 * a + jt + 1)
                        dve.scalar_tensor_tensor(out=p0_lo[:, jt, :], in0=p0[:, jt, :], scalar=z_inv16[:, jt:jt + 1],
                                                 in1=p0_hi[:, jt, :], op0=ALU.mult, op1=ALU.subtract).then_inc(p0_lo_done, 1)
                if it.has("C"):
                    remainder(it, "V1", v_hi_done, 2 * c + 2, v_hi[:, 1, :], v_lo[:, 1, :])
                    split_probs(it, 1)
                if it.has("A"):
                    for r in range(RT):
                        bank, _ = it.pj(f"AT{r}")
                        need(dve, at_relu_done, 2 * a + r + 1)
                        dve.scalar_tensor_tensor(out=leak_part[:, r, :], in0=pj[:, bank, :], scalar=LEAK / WS ** 2,
                                                 in1=x_in[:, r, :], op0=ALU.mult, op1=ALU.add).then_inc(pj_free, 1)
                if it.filling:
                    scale_biases()
                if it.has("C"):
                    masked_scores(it, 2)
                if it.has("A"):
                    stats_of(1, x1, x1_done, (2 * a + 1, 2 * a + 2))
                    carry_wait(1, stats_done[1], 2 * (a + 1))
                    ln_terms_of(1, a)
                if it.has("A"):
                    need(dve, shift_done[1], a + 1)
                    for r in range(RT):
                        dve.tensor_scalar(hn[1][:, r, :], x1[:, r, :], rstd[1][:, r:r + 1], shift[1][:, r:r + 1],
                                          ALU.mult, ALU.add).then_inc(hn_done[1], 1)
                if it.filling:
                    weight_remainders("q")
                if it.has("C"):
                    split_probs(it, 2)
                    masked_scores(it, 3)
                if it.has("A"):
                    split_tr(it, "T1", halves(ht_hi[1]), halves(ht_lo[1]), relu=True)
                if it.has("W"):
                    result(it, 0)
                    result(it, 1)
                if it.has("C"):
                    split_probs(it, 3)
                    need(dve, exp_done, 8 * (c + 1))
                    dve.reciprocal(p_inv[:], p_sum[:]).then_inc(p_inv_done, 1)
                if it.filling:
                    weight_remainders("k", "v")
                    bv_remainder()
                if it.has("N"):
                    stats_of(0, x_in, x_loaded, (16 * (f + 1), 16 * (f + 1)))
                    need(dve, stats_done[0], 2 * (f + 1))
                    need(dve, adj_loaded, 16 * (f + 1))
                    dve.tensor_scalar(mask[it.parity][:], adj_in[:], 0.0, MASKED, ALU.is_le, ALU.mult).then_inc(mask_done, 1)
                    ln_terms_of(0, f)
                if it.has("C"):
                    need(dve, p_inv_done, c + 1)
                    need(dve, o_ready, c + 1)
                    for r in range(RT):
                        dve.tensor_tensor(o_n[:, r, :].rearrange("p (h d) -> p h d", h=NH),
                                          o_ps[:, r, :].rearrange("p (h d) -> p h d", h=NH),
                                          p_inv[:, r, :].unsqueeze(2).to_broadcast([P, NH, DH]), ALU.mult).then_inc(o_n_done, 1)
                if it.has("A"):
                    head_chunks(it, "Q0", q_hi, q_lo, "q", 0, 4 * a + 1)
                if it.has("C"):
                    split_tr(it, "OT", halves(ot_hi), halves(ot_lo))
                if it.has("A"):
                    head_chunks(it, "Q1", q_hi, q_lo, "q", 1, 4 * a + 2)
                    head_chunks(it, "K0", k_hi, k_lo, "k", 0, 4 * a + 3)
                if it.filling:
                    weight_remainders("o")

            every_iteration(dve, body, {-1: lambda: weight_remainders("gat")})


_INS = ["x", "adj", "L0_gnn_W", "L0_gnn_a", "L1_gnn_Wq", "L1_gnn_bq", "L1_gnn_Wk", "L1_gnn_bk", "L1_gnn_Wv", "L1_gnn_bv",
        "L1_gnn_Wo", "L1_gnn_bo"]


def kernel(**inputs):
    import numpy as _np
    import concourse.bacc as _bacc
    from concourse import mybir as _mybir
    from concourse.bass_utils import run_bass_kernel_spmd as _run

    nc = _bacc.Bacc("TRN2", target_bir_lowering=False, num_devices=1)
    arrays, args = {}, []
    for name in _INS:
        a = _np.ascontiguousarray(inputs[name])
        arrays[f"in_{name}_dram"] = a
        args.append(nc.dram_tensor(f"in_{name}_dram", a.shape, _mybir.dt.from_np(a.dtype), kind="ExternalInput").ap())
    shape = arrays["in_x_dram"].shape
    args.append(nc.dram_tensor("out_0_dram", shape, _mybir.dt.float32, kind="ExternalOutput").ap())
    build(nc, *args)
    r = _run(nc, [arrays], core_ids=[0])
    return r.results[0]["out_0_dram"]
```
